# Optimizing a Trainium2 kernel written in Bass

```python
import numpy as np
import jax
import jax.numpy as jnp

def _softmax(x, axis=-1):
    return jax.nn.softmax(x, axis=axis)
def _gelu(x):
    return jax.nn.gelu(x, approximate=True)
def _silu(x):
    return jax.nn.silu(x)
def _sigmoid(x):
    return jax.nn.sigmoid(x)
def _layernorm(x, axis=-1, eps=1e-5):
    m = jnp.mean(x, axis=axis, keepdims=True)
    v = jnp.var(x, axis=axis, keepdims=True)
    return (x - m) / jnp.sqrt(v + eps)
def _scatter_add(tgt, idx, src, axis=0):
    return tgt.at[idx].add(src)
def _segment_sum(src, seg, n):
    return jax.ops.segment_sum(src, seg, n)

kernel_name = 'mk_adj_preln_d4_adj_64_d51e58'

def setup_inputs(seed: int = 0):
    np.random.seed(seed)
    _w = jnp.asarray
    def _rec_inputs():
        import jax
        import jax.numpy as jnp
        _gk = jax.random.key(seed)
        x = -0.0005207 + 1.001 * jax.random.normal(jax.random.fold_in(_gk, 1), (16, 1024, 64), jnp.float32)
        _a = jax.random.bernoulli(jax.random.fold_in(_gk, 2), 0.00390625, (16, 1024, 1024))
        _af = _a.astype(jnp.float32)
        adj = _af
        _nm = jnp.ones((16, 1024), dtype=bool)
        nodemask = _nm
        return x, adj, nodemask
    x, adj, nodemask = _rec_inputs()
    def _L0_gnn_setup():
        import jax, jax.numpy as jnp
        import numpy as np
        B, N, F, U = (16, 2048, 64, 64)
        key = jax.random.key(seed)
        k1, k2, k3 = jax.random.split(key, 3)
        node_features = jax.random.normal(k1, (B, N, F), dtype=jnp.float32)
        adjacency_matrix = (jax.random.uniform(k2, (B, N, N)) < 0.01).astype(jnp.float32)
        kernel = jax.random.normal(k3, (F, U), dtype=jnp.float32) * (1.0 / np.sqrt(F))
        return {'node_features': node_features, 'adjacency_matrix': adjacency_matrix, 'kernel': kernel}
    _L0_gnn_all = _L0_gnn_setup()
    _L0_gnn_in = {k: v for k, v in _L0_gnn_all.items() if k in ('kernel', )}
    del _L0_gnn_all

    def _L1_gnn_setup():
        import jax, jax.numpy as jnp
        import numpy as np
        DEPTH = 3
        DIM = 64
        N_NODES = 4096
        BATCH = 4
        key = jax.random.key(seed)
        k1, k2, k3, k4 = jax.random.split(key, 4)
        x = jax.random.normal(k1, (BATCH, N_NODES, DIM), dtype=jnp.float32)
        graph = jax.random.uniform(k2, (BATCH, N_NODES, N_NODES), dtype=jnp.float32)
        fan_in = (DEPTH + 1) * DIM
        bound = 1.0 / np.sqrt(fan_in)
        W = jax.random.uniform(k3, (DIM, fan_in), minval=-bound, maxval=bound, dtype=jnp.float32)
        b = jax.random.uniform(k4, (DIM,), minval=-bound, maxval=bound, dtype=jnp.float32)
        return {'x': x, 'graph': graph, 'W': W, 'b': b}
    _L1_gnn_all = _L1_gnn_setup()
    _L1_gnn_in = {k: v for k, v in _L1_gnn_all.items() if k in ('W', 'b', )}
    del _L1_gnn_all

    def _L2_gnn_setup():
        import jax, jax.numpy as jnp
        import numpy as np
        TAUS = [0.25, 0.5, 0.75]
        QWEIGHTS = [0.25, 0.5, 0.25]
        T_THRESH = 10
        K_DIL = 2
        EPS_GIN = 0.0

        def _dilate_adj(adj, mask):
            B, N, _ = adj.shape
            eye = jnp.eye(N, dtype=bool)
            adj_ = jnp.where(eye[None], 1.0, adj)
            nb = (adj_ > 0) & (~eye)[None]
            m = nb.sum(-1)
            rank = jnp.cumsum(nb, axis=-1) - 1
            skip = jnp.where(m > T_THRESH, (m + K_DIL - 1) // K_DIL, 1)
            do_dil = (skip > 1) & mask
            removed = nb & do_dil[..., None] & ((rank + 1) % skip[..., None] == 0)
            rem = removed | jnp.swapaxes(removed, 1, 2)
            return jnp.where(rem, 0.0, adj_)

        def _weighted_nanquantile_agg(x, valid):
            B, N, C = x.shape
            big = jnp.finfo(x.dtype).max / 4
            vals = jnp.where(valid[..., None], x[:, None, :, :], big)
            sv = jnp.sort(vals, axis=2)
            m = valid.sum(-1)
            mf = m.astype(x.dtype)

            def gather(idx):
                idxb = jnp.broadcast_to(idx[:, :, None, None], (B, N, 1, C))
                return jnp.take_along_axis(sv, idxb, axis=2)[:, :, 0, :]
            agg = jnp.zeros_like(x)
            for tau, wt in zip(TAUS, QWEIGHTS):
                pos = jnp.clip(tau * (mf - 1.0), 0.0)
                lo = jnp.floor(pos).astype(jnp.int32)
                hi = jnp.ceil(pos).astype(jnp.int32)
                frac = (pos - lo.astype(x.dtype))[..., None]
                q = gather(lo) * (1.0 - frac) + gather(hi) * frac
                agg = agg + wt * q
            return jnp.where((m > 0)[..., None], agg, 0.0)
        key = jax.random.key(seed)
        k0, k1, k2, k3 = jax.random.split(key, 4)
        B, N, C, H, CO = (4, 512, 64, 128, 64)
        x = jax.random.normal(k0, (B, N, C), dtype=jnp.float32)
        u = jax.random.uniform(k1, (B, N, N))
        a = (u < 0.03).astype(jnp.float32)
        adj = jnp.maximum(a, jnp.swapaxes(a, 1, 2))
        mask = jnp.broadcast_to(jnp.arange(N) < N - 32, (B, N))
        W1 = jax.random.normal(k2, (C, H), dtype=jnp.float32) * (1.0 / np.sqrt(C))
        b1 = jnp.zeros((H,), dtype=jnp.float32)
        W2 = jax.random.normal(k3, (H, CO), dtype=jnp.float32) * (1.0 / np.sqrt(H))
        b2 = jnp.zeros((CO,), dtype=jnp.float32)
        return {'x': x, 'adj': adj, 'mask': mask, 'W1': W1, 'b1': b1, 'W2': W2, 'b2': b2}
    _L2_gnn_all = _L2_gnn_setup()
    _L2_gnn_in = {k: v for k, v in _L2_gnn_all.items() if k in ('W1', 'b1', 'W2', 'b2', )}
    del _L2_gnn_all

    def _L3_gnn_setup():
        import jax, jax.numpy as jnp
        import numpy as np
        B, L, F = (8, 4096, 64)
        key = jax.random.key(seed)
        k1, k2, k3, k4 = jax.random.split(key, 4)
        text = jax.random.normal(k1, (B, L, F), dtype=jnp.float32)
        adj = jax.random.uniform(k2, (B, L, L), dtype=jnp.float32)
        weight = jax.random.normal(k3, (F, F), dtype=jnp.float32) * (1.0 / np.sqrt(F))
        bias = jax.random.normal(k4, (F,), dtype=jnp.float32) * 0.01
        return {'text': text, 'adj': adj, 'weight': weight, 'bias': bias}
    _L3_gnn_all = _L3_gnn_setup()
    _L3_gnn_in = {k: v for k, v in _L3_gnn_all.items() if k in ('weight', 'bias', )}
    del _L3_gnn_all

    return {
        "x": x,
        "adj": adj,
        "nodemask": nodemask,
        "L0_gnn_kernel": _L0_gnn_in["kernel"],
        "L1_gnn_W": _L1_gnn_in["W"],
        "L1_gnn_b": _L1_gnn_in["b"],
        "L2_gnn_W1": _L2_gnn_in["W1"],
        "L2_gnn_b1": _L2_gnn_in["b1"],
        "L2_gnn_W2": _L2_gnn_in["W2"],
        "L2_gnn_b2": _L2_gnn_in["b2"],
        "L3_gnn_weight": _L3_gnn_in["weight"],
        "L3_gnn_bias": _L3_gnn_in["bias"],
    }

def reference(x, adj, nodemask, L0_gnn_kernel, L1_gnn_W, L1_gnn_b, L2_gnn_W1, L2_gnn_b1, L2_gnn_W2, L2_gnn_b2, L3_gnn_weight, L3_gnn_bias):
    import jax
    import jax.numpy as jnp
    def _L0_gnn_ref(node_features, adjacency_matrix, kernel):
        import jax, jax.numpy as jnp
        import numpy as np
        B, N, F, U = (16, 2048, 64, 64)
        n = adjacency_matrix.shape[-1]
        adj = adjacency_matrix + jnp.eye(n, dtype=adjacency_matrix.dtype)
        row_sum = jnp.sum(adj, axis=-1)
        d_inv_sqrt = jnp.where(row_sum > 0, row_sum ** (-0.5), 0.0)
        norm_adj = d_inv_sqrt[:, :, None] * adj * d_inv_sqrt[:, None, :]
        transformed = jnp.einsum('bnf,fu->bnu', node_features, kernel)
        out = jnp.einsum('bnm,bmu->bnu', norm_adj, transformed)
        return jax.nn.relu(out)

    def _L1_gnn_ref(x, graph, W, b):
        import jax, jax.numpy as jnp
        import numpy as np
        DEPTH = 3
        DIM = 64
        N_NODES = 4096
        BATCH = 4
        n = graph.shape[-1]
        g = graph + jnp.eye(n, dtype=graph.dtype)
        d = 1.0 / (jnp.sqrt(g.sum(axis=-1)) + 1e-07)
        g = g * d[..., :, None] * d[..., None, :]
        outs = [x]
        h = x
        for _ in range(DEPTH):
            h = jnp.einsum('bij,bjd->bid', g, h)
            outs.append(h)
        cat = jnp.concatenate(outs, axis=-1)
        return cat @ W.T + b

    def _L2_gnn_ref(x, adj, mask, W1, b1, W2, b2):
        import jax, jax.numpy as jnp
        import numpy as np
        TAUS = [0.25, 0.5, 0.75]
        QWEIGHTS = [0.25, 0.5, 0.25]
        T_THRESH = 10
        K_DIL = 2
        EPS_GIN = 0.0

        def _dilate_adj(adj, mask):
            B, N, _ = adj.shape
            eye = jnp.eye(N, dtype=bool)
            adj_ = jnp.where(eye[None], 1.0, adj)
            nb = (adj_ > 0) & (~eye)[None]
            m = nb.sum(-1)
            rank = jnp.cumsum(nb, axis=-1) - 1
            skip = jnp.where(m > T_THRESH, (m + K_DIL - 1) // K_DIL, 1)
            do_dil = (skip > 1) & mask
            removed = nb & do_dil[..., None] & ((rank + 1) % skip[..., None] == 0)
            rem = removed | jnp.swapaxes(removed, 1, 2)
            return jnp.where(rem, 0.0, adj_)

        def _weighted_nanquantile_agg(x, valid):
            B, N, C = x.shape
            big = jnp.finfo(x.dtype).max / 4
            vals = jnp.where(valid[..., None], x[:, None, :, :], big)
            sv = jnp.sort(vals, axis=2)
            m = valid.sum(-1)
            mf = m.astype(x.dtype)

            def gather(idx):
                idxb = jnp.broadcast_to(idx[:, :, None, None], (B, N, 1, C))
                return jnp.take_along_axis(sv, idxb, axis=2)[:, :, 0, :]
            agg = jnp.zeros_like(x)
            for tau, wt in zip(TAUS, QWEIGHTS):
                pos = jnp.clip(tau * (mf - 1.0), 0.0)
                lo = jnp.floor(pos).astype(jnp.int32)
                hi = jnp.ceil(pos).astype(jnp.int32)
                frac = (pos - lo.astype(x.dtype))[..., None]
                q = gather(lo) * (1.0 - frac) + gather(hi) * frac
                agg = agg + wt * q
            return jnp.where((m > 0)[..., None], agg, 0.0)
        dtp = x.dtype
        adj_d = _dilate_adj(adj, mask)
        agg = _weighted_nanquantile_agg(x, adj_d > 0)
        out = (1.0 + EPS_GIN) * x + agg
        h = jax.nn.relu(jnp.einsum('bnc,ch->bnh', out, W1) + b1)
        y = jnp.einsum('bnh,ho->bno', h, W2) + b2
        return y * mask[..., None].astype(dtp)

    def _L3_gnn_ref(text, adj, weight, bias):
        import jax, jax.numpy as jnp
        import numpy as np
        B, L, F = (8, 4096, 64)
        hidden = jnp.einsum('blf,fo->blo', text, weight)
        out = jnp.einsum('bij,bjo->bio', adj, hidden)
        return out + bias

    h = jnp.maximum(_layernorm(x, axis=-1), 0.0)
    x = x + _L0_gnn_ref(h, adj, L0_gnn_kernel)
    h = jnp.maximum(_layernorm(x, axis=-1), 0.0)
    x = x + _L1_gnn_ref(h, adj, L1_gnn_W, L1_gnn_b)
    h = jnp.maximum(_layernorm(x, axis=-1), 0.0)
    x = x + _L2_gnn_ref(h, adj, nodemask, L2_gnn_W1, L2_gnn_b1, L2_gnn_W2, L2_gnn_b2)
    h = jnp.maximum(_layernorm(x, axis=-1), 0.0)
    x = x + _L3_gnn_ref(h, adj, L3_gnn_weight, L3_gnn_bias)
    return x


_drawn_inputs = setup_inputs


def setup_inputs(seed=0):
    import zlib

    import numpy as np

    out = dict(_drawn_inputs(seed))
    spreads = {'L2_gnn_b1': (0.0, 0.1), 'L2_gnn_b2': (0.0, 0.1)}
    factors = {'L3_gnn_bias': 8.0}
    for name, (base, spread) in spreads.items():
        noise = np.random.default_rng([zlib.crc32(name.encode()), seed]).standard_normal(out[name].shape)
        drawn = base * np.exp(spread * noise) if base else spread * noise
        out[name] = jnp.asarray(drawn.astype(out[name].dtype))
    for name, factor in factors.items():
        out[name] = (out[name] * factor).astype(out[name].dtype)
    return out
```

```python
from contextlib import ExitStack

import concourse.bass as bass
from concourse import mybir

NETWORK = [
    [(i, i + 1) for i in range(0, 16, 2)],
    [(0, 2), (4, 6), (8, 10), (12, 14), (1, 3), (5, 7), (9, 11), (13, 15)],
    [(0, 4), (8, 12), (1, 5), (9, 13), (2, 6), (10, 14), (3, 7), (11, 15)],
    [(i, i + 8) for i in range(8)],
    [(5, 10), (6, 9), (3, 12), (13, 14), (7, 11), (1, 2), (4, 8)],
    [(1, 4), (7, 13), (2, 8), (11, 14)],
    [(2, 4), (5, 6), (9, 10), (11, 13), (3, 8), (7, 12)],
    [(6, 8), (10, 12), (3, 5), (7, 9)],
    [(3, 4), (5, 6), (7, 8), (9, 10), (11, 12)],
    [(6, 7), (8, 9)],
]
SLOTS = 16
T_THRESH = 10
ROUND = 8388608.0


def pruned(network, wanted):
    live, out = set(wanted), []
    for layer in reversed(network):
        out.append([(a, b, a in live, b in live) for a, b in layer if a in live or b in live])
        live |= {i for a, b, _, _ in out[-1] for i in (a, b)}
    return out[::-1]


class Steps:

    def __init__(self, engine, sem):
        self.engine, self.sem, self.n = engine, sem, 0

    def restart(self):
        self.wait()
        self.engine.sem_clear(self.sem)
        self.n = 0

    def done(self, ins):
        ins.then_inc(self.sem, 1)
        self.n += 1

    def wait(self, lag=0):
        if self.n > lag:
            self.engine.wait_ge(self.sem, self.n - lag)


def at_least(engine, sem, value):
    if isinstance(value, int) and value <= 0:
        return
    engine.wait_ge(sem, value)


def gnn_stack(nc, x_in, adj, nodemask, w_l0, w_l1, b_l1, w1, b1, w2, b2, w_l3, b_l3, out, limit=SLOTS - 1):
    f32, bf16, f16 = mybir.dt.float32, mybir.dt.bfloat16, mybir.dt.float16
    i32, u8 = mybir.dt.int32, mybir.dt.uint8
    ALU, ACT, AX = mybir.AluOpType, mybir.ActivationFunctionType, mybir.AxisListType

    B, N, C = x_in.shape
    P = 128
    T = N // P
    H = w1.shape[1]
    HALF = N // 2
    F = T * C
    DEPTH = 3
    EPS = 1e-5
    RING = 4
    DIAG = N + P

    x_v = x_in.rearrange("b (t p) c -> b p t c", p=P)
    out_v = out.rearrange("b (t p) c -> b p t c", p=P)
    adj_v = adj.rearrange("b (t p) m -> b t p m", p=P)

    ctx = ExitStack()
    with ctx:
        def sb(name, shape, dt):
            return ctx.enter_context(nc.sbuf_tensor(name, shape, dt))

        def pb(name, shape, dt):
            return ctx.enter_context(nc.psum_tensor(name, shape, dt))

        def sem(name):
            return ctx.enter_context(nc.semaphore(name))

        ident_f = sb("ident_f", [P, P], f32)
        ident_b = sb("ident_b", [P, P], bf16)
        ident_h = sb("ident_h", [P, P], f16)
        off_diag = sb("off_diag", [P, P], bf16)
        prefix = sb("prefix", [P, N], bf16)
        ones_col = sb("ones_col", [P, 1], bf16)
        ranks = sb("ranks", [P, SLOTS], f32)
        quant_w = sb("quant_w", [P, 3], f32)
        eps_col = sb("eps_col", [P, 1], f32)
        w_l0_sb = sb("w_l0_sb", [C, C], f32)
        w_l1_sb = sb("w_l1_sb", [C, (DEPTH + 1) * C], f32)
        w1_sb = sb("w1_sb", [C, H], f32)
        b1_sb = sb("b1_sb", [H, 1], f32)
        w2_sb = sb("w2_sb", [H, C], f32)
        w_l3_sb = sb("w_l3_sb", [C, C], f32)
        bias_l1 = sb("bias_l1", [P, C], f32)
        bias_l2 = sb("bias_l2", [P, C], f32)
        bias_l3 = sb("bias_l3", [P, C], f32)
        mask_raw = sb("mask_raw", [B * T, P], u8)
        mask = sb("mask", [P, B, T], f32)
        mask_g = sb("mask_g", [P, T], f32)

        adj_f = sb("adj_f", [P, RING, N], f32)
        adj_n = sb("adj_n", [P, T * N], bf16)
        adj_t = sb("adj_t", [P, T * N], bf16)
        nbr_diag = sb("nbr_diag", [P, T, P], bf16)
        cum = sb("cum", [P, T * N], f16)
        keep = sb("keep", [P, T * N], f16)
        pos_t = sb("pos_t", [P, T * N], f16)
        one_hot = [sb(f"one_hot{i}", [P, T * N], bf16) for i in range(2)]
        valid_t = one_hot[0]

        x = sb("x", [P, F], f32)
        h = sb("h", [P, F], f32)
        y = sb("y", [P, F], f32)
        sq = y
        res = sb("res", [P, F], f32)
        mask_rows = res[0:B * T, 0:P]
        xc = res
        parts = sb("parts", [P, T, 3 * C], bf16)
        h_t = sb("h_t", [C, N], f32)
        g_l1 = sb("g_l1", [P, T, (DEPTH + 1) * C], f32)
        w_l1_rows = y[0:C, 0:(DEPTH + 1) * C]
        slots = sb("slots", [P, (SLOTS + 4) * F], f32)
        slot = [slots[:, i * F:(i + 1) * F] for i in range(SLOTS + 4)]
        hid_t = slots[0:H, 0:N]
        agg = sb("agg", [P, F], f32)
        stat = sb("stat", [P, 8, T], f32)
        deg, d0, d1, s_sum, s_var, s_std, s_rstd, root = [stat[:, i, :] for i in range(8)]
        dil = sb("dil", [P, 8, T], f32)
        m_all, m_skip, m_do, m_drop1, m_drop2, m_cnt, m_t, m_max = [dil[:, i, :] for i in range(8)]
        over = sb("over", [P, T], f32)
        flag = sb("flag", [P, 1], i32)
        q_pos = sb("q_pos", [P, 3, T], f32)
        hat = sb("hat", [P, 2, 3 * T * SLOTS], f32)
        w_rank = sb("w_rank", [P, T, SLOTS], f32)

        q_hi = sb("q_hi", [P, 3, T], f32)
        q_frac = sb("q_frac", [P, 3, T], f32)
        col = sb("col", [P, T], f32)
        col_agg = sb("col_agg", [P, T], f32)
        q_val = sb("q_val", [P, 2, 3], f32)

        ps_tr = [pb(f"ps_tr{i}", [P, HALF], f32) for i in range(2)]
        ps_cum = pb("ps_cum", [P, N], f32)
        ps_prod = pb("ps_prod", [P, F], f32)
        ps_gat = pb("ps_gat", [P, 2, HALF], f32)
        ps_misc = pb("ps_misc", [P, HALF], f32)

        const_in = sem("const_in")
        const_pool = sem("const_pool")
        const_pe = sem("const_pe")
        const_v = sem("const_v")
        x_loaded = sem("x_loaded")
        adj_loaded = [sem(f"adj_loaded{i}") for i in range(RING)]
        cast_done = sem("cast_done")
        tr_full, tr_free = sem("tr_full"), sem("tr_free")
        cum_full, cum_free = sem("cum_full"), sem("cum_free")
        prod_full = sem("prod_full")
        gat_full, gat_free = sem("gat_full"), sem("gat_free")
        misc_full = sem("misc_full")
        misc_read_act = sem("misc_read_act")
        nbr_ready = sem("nbr_ready")
        thresholds_ready = sem("thresholds_ready")
        weights_ready = sem("weights_ready")
        hi_ready, mid_ready = sem("hi_ready"), sem("mid_ready")
        std_ready, root_ready = sem("std_ready"), sem("root_ready")
        var_ready, y_ready, res_ready = sem("var_ready"), sem("y_ready"), sem("res_ready")
        slow_to_pe, slow_to_v = sem("slow_to_pe"), sem("slow_to_v")
        v_step, pool_step = sem("v_step"), sem("pool_step")
        v_mark = sem("v_mark")
        slow_step = sem("slow_step")
        out_done = sem("out_done")
        settled = sem("settled")

        def tiles(a):
            return a[:, :].rearrange("p (t c) -> p t c", t=T)

        def over_c(s):
            return s.unsqueeze(2).to_broadcast([P, T, C])

        def over_t(row):
            return row.unsqueeze(1).to_broadcast([P, T, C])

        TR = 3 * T
        assert TR == 2 * T + 8
        PROD = 5
        GAT = SLOTS
        MISC = 1 + T // 2 + 3 + 1
        MISC_ACT = T // 2 + 2
        SPLIT = [y, y, y, y, h, y]

        V = {}
        for name in (["h0", "parts0"] + [f"pos{t}" for t in range(T)] + ["prod0_read", "h1"]
                     + ["parts1", "prod1_read", "parts2", "prod2_read", "parts3", "prod3_read", "h2", "parts_h2",
                        "valid"] + [f"hot{k}" for k in range(1, SLOTS)]
                     + ["sorted", "mlp_in", "y_read", "h3", "w3_read", "parts_l3", "prod_l3_read", "result"]):
            V[name] = len(V) + 1
        VM = len(V)

        def marked(engine, g, name):
            at_least(engine, v_mark, g * VM + V[name])

        def settle(engine):
            engine.sem_inc(settled, 1)

        block = ctx.enter_context(nc.Block())

        @block.sync
        def _(sp):
            for dst, src in [(w_l0_sb[:, :], w_l0), (w_l1_rows[:, :], w_l1), (w1_sb[:, :], w1),
                             (b1_sb[:, :], b1.unsqueeze(1)), (w2_sb[:, :], w2), (w_l3_sb[:, :], w_l3),
                             (bias_l1[:, :], b_l1.partition_broadcast(P)), (bias_l2[:, :], b2.partition_broadcast(P)),
                             (bias_l3[:, :], b_l3.partition_broadcast(P)),
                             (mask_raw[:, :], nodemask.rearrange("b (t p) -> (b t) p", p=P))]:
                sp.dma_start(dst, src).then_inc(const_in, 16)

            def load(g):
                if not (isinstance(g, int) and g == 0):
                    sp.wait_ge(out_done, g * 16)
                sp.dma_start(tiles(x), x_v[g]).then_inc(x_loaded, 16)

            def load_adj(g):
                for t in range(T):
                    at_least(sp, cast_done, g * T + (t + 1 - RING))
                    sp.dma_start(adj_f[:, t % RING, :], adj_v[g, t]).then_inc(adj_loaded[t % RING], 16)

            load(0)
            load_adj(0)
            if B > 1:
                with sp.Fori(1, B) as g:
                    load_adj(g)
                    marked(sp, g - 1, "result")
                    sp.dma_start(out_v[g - 1], tiles(x)).then_inc(out_done, 16)
                    load(g)
            marked(sp, B - 1, "result")
            sp.dma_start(out_v[B - 1], tiles(x)).then_inc(out_done, 16)
            sp.wait_ge(out_done, 16 * B)

        @block.gpsimd
        def _(pool):
            st = Steps(pool, pool_step)

            def step(ins):
                st.done(ins)
                st.wait()

            for m in (ident_f, ident_b, ident_h):
                step(pool.memset(m[:, :], 0.0))
                step(pool.affine_select(out=m[:, :], in_=m[:, :], compare_op=ALU.not_equal, fill=1.0, base=0,
                                        pattern=[[-1, P]], channel_multiplier=1))
            step(pool.memset(off_diag[:, :], 1.0))
            step(pool.affine_select(out=off_diag[:, :], in_=off_diag[:, :], compare_op=ALU.not_equal, fill=0.0,
                                    base=0, pattern=[[-1, P]], channel_multiplier=1))
            step(pool.memset(prefix[:, :], 1.0))
            step(pool.affine_select(out=prefix[:, 0:P], in_=prefix[:, 0:P], compare_op=ALU.is_ge, fill=0.0, base=0,
                                    pattern=[[1, P]], channel_multiplier=-1))
            step(pool.memset(ones_col[:, :], 1.0))
            step(pool.memset(eps_col[:, :], EPS))
            for r in range(SLOTS):
                step(pool.memset(ranks[:, r:r + 1], float(r)))
            for q, w in enumerate((0.25, 0.5, 0.25)):
                step(pool.memset(quant_w[:, q:q + 1], w))
            pool.wait_ge(const_in, 160)
            step(pool.tensor_copy(mask_rows[:, :], mask_raw[:, :]))
            pool.sem_inc(const_pool, 1)

            def diagonals(dst, src, factor, op):
                rows = src[:, 0:(T - 1) * DIAG].rearrange("p (t s) -> p t s", s=DIAG)[:, :, 0:P]
                to = dst[0] if isinstance(dst, tuple) else dst[:, 0:(T - 1) * DIAG].rearrange(
                    "p (t s) -> p t s", s=DIAG)[:, :, 0:P]
                last = dst[1] if isinstance(dst, tuple) else dst[:, (T - 1) * DIAG:T * N]
                st.done(pool.tensor_tensor(to, rows, factor[:, :].unsqueeze(1).to_broadcast([P, T - 1, P]), op))
                st.done(pool.tensor_tensor(last, src[:, (T - 1) * DIAG:T * N], factor[:, :], op))

            def graph(g):
                pool.wait_ge(tr_full, g * TR + T)
                diagonals(adj_n, adj_n, off_diag, ALU.mult)
                pool.wait_ge(tr_free, g * TR + T)
                diagonals((nbr_diag[:, 0:T - 1, :], nbr_diag[:, T - 1, :]), adj_t, off_diag, ALU.mult)
                st.wait()
                pool.sem_inc(nbr_ready, 1)

                pool.wait_ge(cum_free, (g + 1) * T)
                settle(pool)
                step(pool.tensor_copy(m_all, cum[:, :].rearrange("p (t n) -> p t n", t=T)[:, :, N - 1]))
                step(pool.tensor_copy(mask_g[:, :], mask[:, g, :]))
                step(pool.tensor_scalar(m_skip, m_all, 0.5, 0.25, ALU.mult, ALU.add))
                step(pool.tensor_scalar(m_skip, m_skip, ROUND, ROUND, ALU.add, ALU.subtract))
                step(pool.tensor_scalar(m_do, m_all, float(T_THRESH), None, ALU.is_gt))
                step(pool.tensor_tensor(m_do, m_do, mask_g[:, :], ALU.mult))
                step(pool.tensor_tensor(m_skip, m_skip, m_do, ALU.mult))
                step(pool.tensor_tensor(m_skip, m_skip, m_do, ALU.add))
                step(pool.tensor_scalar(m_drop1, m_skip, -1.0, None, ALU.add))
                step(pool.tensor_scalar(m_drop2, m_drop1, 2.0, None, ALU.mult))
                pool.sem_inc(thresholds_ready, 1)
                step(pool.tensor_scalar(m_max, m_all, float(limit), None, ALU.is_gt))
                step(pool.partition_all_reduce(over[:, :], m_max, P, bass.bass_isa.ReduceOp.add))
                w = T // 2
                while w:
                    step(pool.tensor_tensor(over[:, 0:w], over[:, 0:w], over[:, w:2 * w], ALU.add))
                    w //= 2
                step(pool.tensor_scalar(over[:, 0:1], over[:, 0:1], 0.0, None, ALU.is_gt))
                step(pool.tensor_copy(flag[:, :], over[:, 0:1]))

                pool.wait_ge(gat_free, g * GAT + 1)
                settle(pool)
                for q, tau in enumerate((0.25, 0.5, 0.75)):
                    step(pool.tensor_scalar(q_pos[:, q, :], m_cnt, tau, None, ALU.mult))
                a = hat[:, 0, :].rearrange("p (t r) -> p t r", r=SLOTS)
                c = hat[:, 1, :].rearrange("p (t r) -> p t r", r=SLOTS)
                step(pool.tensor_tensor(a, ranks[:, :].unsqueeze(1).to_broadcast([P, 3 * T, SLOTS]),
                                        q_pos[:, :, :].rearrange("p q t -> p (q t)").unsqueeze(2)
                                        .to_broadcast([P, 3 * T, SLOTS]), ALU.subtract))
                step(pool.tensor_scalar(c, a, 0.0, None, ALU.max))
                step(pool.tensor_scalar(a, a, 0.0, None, ALU.min))
                step(pool.tensor_tensor(a, a, c, ALU.subtract))
                step(pool.tensor_scalar(a, a, 1.0, None, ALU.add))
                step(pool.tensor_scalar(a, a, 0.0, 0.25, ALU.max, ALU.mult))
                a4 = hat[:, 0, :].rearrange("p (q t r) -> p q t r", q=3, r=SLOTS)
                step(pool.tensor_tensor(w_rank[:, :, :], a4[:, 0], a4[:, 2], ALU.add))
                step(pool.tensor_tensor(w_rank[:, :, :], w_rank[:, :, :], a4[:, 1], ALU.add))
                step(pool.tensor_tensor(w_rank[:, :, :], w_rank[:, :, :], a4[:, 1], ALU.add))
                pool.sem_inc(weights_ready, 1)
                st.restart()

            st.restart()
            graph(0)
            if B > 1:
                with pool.Fori(1, B) as g:
                    marked(pool, g - 1, "h3")
                    graph(g)

        @block.scalar
        def _(act):
            act.wait_ge(const_pool, 1)
            act.wait_ge(const_pe, 2)
            act.activation(mask[:, :, :].rearrange("p b t -> p (b t)"), ps_misc[:, 0:B * T], ACT.Copy)\
               .then_inc(misc_read_act, 1)
            act.activation(w_l1_sb[:, :], ps_prod[0:C, 0:(DEPTH + 1) * C], ACT.Copy).then_inc(misc_read_act, 1)

            def graph(g):
                tr = [g * TR]

                def from_tr(dst, bank_view):
                    tr[0] += 1
                    n = tr[0]
                    act.wait_ge(tr_full, n)
                    act.activation(dst, bank_view, ACT.Copy).then_inc(tr_free, 1)

                def square_tiles(dst, t):
                    return dst[:, :].rearrange("p (j n) -> p j n", j=T)[:, :, t * P:(t + 1) * P]

                def std(i):
                    marked_std = g * 4 + i + 1
                    act.wait_ge(var_ready, marked_std)
                    act.activation(s_std, s_var, ACT.Sqrt, bias=eps_col[:, :], scale=1.0 / C).then_inc(std_ready, 1)

                def split(i):
                    act.wait_ge(y_ready, g * 6 + i + 1)
                    act.activation(parts[:, :, 0:C], tiles(SPLIT[i]), ACT.Copy).then_inc(hi_ready, 1)
                    act.wait_ge(res_ready, g * 6 + i + 1)
                    act.activation(parts[:, :, C:2 * C], tiles(res), ACT.Copy).then_inc(mid_ready, 1)

                def feature_rows():
                    for i in range(2):
                        from_tr(h_t[:, i * HALF:(i + 1) * HALF], ps_tr[i][0:C, :])

                for t in range(T):
                    act.wait_ge(adj_loaded[t % RING], g * (T // RING * 16) + (t // RING + 1) * 16)
                    if t == 0 and not isinstance(g, int):
                        marked(act, g - 1, "valid")
                    act.activation(adj_n[:, t * N:(t + 1) * N], adj_f[:, t % RING, :], ACT.Copy, accum_out=deg[:, t:t + 1])\
                       .then_inc(cast_done, 1)
                act.wait_ge(cast_done, (g + 1) * T)
                act.activation(root, deg, ACT.Sqrt, bias=1.0).then_inc(root_ready, 1)
                if not isinstance(g, int):
                    marked(act, g - 1, "prod_l3_read")
                for t in range(T):
                    from_tr(square_tiles(adj_t, t),
                            ps_tr[t % 2][:, :].bitcast(bf16).rearrange("p (j n) -> p j n", j=T))
                std(0)
                feature_rows()
                for t in range(T):
                    act.wait_ge(cum_full, g * T + t + 1)
                    act.activation(cum[:, t * N:(t + 1) * N], ps_cum[:, :], ACT.Copy).then_inc(cum_free, 1)
                split(0)
                for t in range(T):
                    from_tr(square_tiles(pos_t, t),
                            ps_tr[t % 2][:, :].bitcast(f16).rearrange("p (j n) -> p j n", j=T))
                std(1)
                feature_rows()
                for i in range(T // 2):
                    act.wait_ge(misc_full, g * MISC + 2 + i)
                    act.activation(g_l1[:, 2 * i:2 * i + 2, :],
                                   ps_misc[:, :].rearrange("p (t c) -> p t c", t=2), ACT.Copy)\
                       .then_inc(misc_read_act, 1)
                for i in (1, 2, 3):
                    split(i)
                std(2)
                split(4)
                act.wait_ge(gat_full, g * GAT + 1)
                if not isinstance(g, int):
                    marked(act, g - 1, "sorted")
                act.activation(m_cnt, ps_gat[:, 0, 0:T], ACT.Copy).then_inc(gat_free, 1)
                for k in range(1, SLOTS):
                    act.wait_ge(gat_full, g * GAT + k + 1)
                    act.activation(slot[k - 1][:, :], ps_gat[:, k % 2, :], ACT.Copy).then_inc(gat_free, 1)
                feature_rows()
                for i in range(2):
                    act.wait_ge(misc_full, g * MISC + 2 + T // 2 + i)
                    act.activation(hid_t[:, i * HALF:(i + 1) * HALF], ps_misc[:, :], ACT.Relu, bias=b1_sb[:, :])\
                       .then_inc(misc_read_act, 1)
                std(3)
                feature_rows()
                split(5)

            graph(0)
            if B > 1:
                with act.Fori(1, B) as g:
                    graph(g)

        @block.tensor
        def _(pe):
            pe.wait_ge(const_pool, 1)
            nc.tensor.transpose(ps_misc[:, 0:B * T], mask_rows[:, :], ident_f[0:B * T, 0:B * T]).then_inc(const_pe, 1)
            for i in range(DEPTH + 1):
                last = nc.tensor.transpose(ps_prod[0:C, i * C:(i + 1) * C], w_l1_rows[:, i * C:(i + 1) * C],
                                           ident_f[0:C, 0:C])
            last.then_inc(const_pe, 1)
            pe.wait_ge(misc_read_act, 2)

            def graph(g):
                tr = [0]

                def tr_bank():
                    at_least(pe, tr_free, g * TR + tr[0] - 1)
                    bank = ps_tr[tr[0] % 2]
                    tr[0] += 1
                    return bank

                def transpose_tile(src, t, ident, dt):
                    bank = tr_bank()
                    view = bank[:, :].bitcast(dt).rearrange("p (j n) -> p j n", j=T)
                    for j in range(T):
                        last = nc.tensor.transpose(view[:, j, :], src[:, t * N + j * P:t * N + (j + 1) * P],
                                                   ident[:, :])
                    last.then_inc(tr_full, 1)

                def transpose_features(src):
                    for i in range(2):
                        bank = tr_bank()
                        settle(pe)
                        for t in range(T // 2):
                            tt = i * (T // 2) + t
                            last = nc.tensor.transpose(bank[0:C, t * P:(t + 1) * P], src[:, tt * C:(tt + 1) * C],
                                                       ident_f[:, :])
                        last.then_inc(tr_full, 1)

                def rows_ready():
                    pe.wait_ge(tr_free, g * TR + tr[0])

                def product(dst, lhs_t, signal):
                    for t in range(T):
                        for j in range(T):
                            for k in range(3):
                                last = nc.tensor.matmul(dst[:, t * C:(t + 1) * C],
                                                        lhs_t[:, j * N + t * P:j * N + (t + 1) * P],
                                                        parts[:, j, k * C:(k + 1) * C],
                                                        start=(j == 0 and k == 0), stop=(j == T - 1 and k == 2))
                    last.then_inc(signal, 1)

                def node_linear(w_sb, width):
                    for t in range(T):
                        last = nc.tensor.matmul(ps_misc[:, t * width:(t + 1) * width], h_t[:, t * P:(t + 1) * P],
                                                w_sb[:, :], start=True, stop=True)
                    last.then_inc(misc_full, 1)

                def ranks_of(t):
                    at_least(pe, cum_free, g * T + t)
                    for half in range(2):
                        lo = half * HALF
                        js = [j for j in range(T) if j * P < lo + HALF]
                        for j in js:
                            start = max(lo, j * P)
                            lhs = nbr_diag[:, t, :] if j == t else adj_t[:, j * N + t * P:j * N + (t + 1) * P]
                            last = nc.tensor.matmul(ps_cum[:, start:lo + HALF], lhs,
                                                    prefix[:, start - j * P:lo + HALF - j * P],
                                                    start=(j == 0), stop=(j == js[-1]))
                    last.then_inc(cum_full, 1)

                for t in range(T):
                    pe.wait_ge(cast_done, g * T + t + 1)
                    transpose_tile(adj_n, t, ident_b, bf16)
                marked(pe, g, "h0")
                transpose_features(h)
                rows_ready()
                if not isinstance(g, int):
                    marked(pe, g - 1, "w3_read")
                node_linear(w_l0_sb, C)
                pe.wait_ge(nbr_ready, g + 1)
                for t in range(T):
                    ranks_of(t)
                marked(pe, g, "parts0")
                if not isinstance(g, int):
                    marked(pe, g - 1, "prod_l3_read")
                product(ps_prod, adj_t, prod_full)
                for t in range(T):
                    marked(pe, g, f"pos{t}")
                    transpose_tile(cum, t, ident_h, f16)
                marked(pe, g, "h1")
                transpose_features(h)
                rows_ready()
                for i in range(T // 2):
                    if i:
                        pe.wait_ge(misc_read_act, 2 + g * MISC_ACT + i)
                    for t in range(2):
                        tt = 2 * i + t
                        last = nc.tensor.matmul(ps_misc[:, t * 4 * C:(t + 1) * 4 * C], h_t[:, tt * P:(tt + 1) * P],
                                                w_l1_sb[:, :], start=True, stop=True)
                    last.then_inc(misc_full, 1)
                for i in (1, 2, 3):
                    marked(pe, g, f"parts{i}")
                    product(ps_prod, adj_t, prod_full)
                marked(pe, g, "valid")
                at_least(pe, gat_free, (g - 1) * GAT + GAT - 1)
                for t in range(T):
                    for j in range(T):
                        last = nc.tensor.matmul(ps_gat[:, 0, t:t + 1], valid_t[:, j * N + t * P:j * N + (t + 1) * P],
                                                ones_col[:, :], start=(j == 0), stop=(j == T - 1))
                last.then_inc(gat_full, 1)
                for k in range(1, SLOTS):
                    marked(pe, g, f"hot{k}")
                    at_least(pe, gat_free, g * GAT + k - 1)
                    product(ps_gat[:, k % 2, :], one_hot[k % 2], gat_full)
                slow_pe(pe, g)
                marked(pe, g, "mlp_in")
                transpose_features(agg)
                rows_ready()
                for i in range(2):
                    pe.wait_ge(misc_read_act, 2 + g * MISC_ACT + T // 2 + i)
                    nc.tensor.matmul(ps_misc[:, :], w1_sb[:, :], h_t[:, i * HALF:(i + 1) * HALF],
                                     start=True, stop=True).then_inc(misc_full, 1)
                pe.wait_ge(misc_read_act, 2 + (g + 1) * MISC_ACT)
                for t in range(T):
                    last = nc.tensor.matmul(ps_misc[:, t * C:(t + 1) * C], hid_t[:, t * P:(t + 1) * P], w2_sb[:, :],
                                            start=True, stop=True)
                last.then_inc(misc_full, 1)
                marked(pe, g, "h3")
                transpose_features(h)
                rows_ready()
                node_linear(w_l3_sb, C)
                marked(pe, g, "parts_l3")
                product(ps_prod, adj_t, prod_full)
                assert tr[0] == TR

            def slow_pe(pe, g):
                pe.wait_ge(weights_ready, g + 1)
                settle(pe)
                many = pe.value_load(flag[0:1, 0:1], min_val=0, max_val=1)
                with pe.If(many > 0):
                    with pe.Fori(0, C) as c:
                        pe.wait_ge(slow_to_pe, c * (T + 2) + 1)
                        for t in range(T):
                            last = nc.tensor.transpose(ps_gat[:, t // (T // 2), (t % (T // 2)) * P:(t % (T // 2) + 1) * P],
                                                       col[:, t:t + 1].to_broadcast([P, P]), ident_f[:, :])
                        last.then_inc(slow_to_v, 1)
                        for t in range(T):
                            pe.wait_ge(slow_to_pe, c * (T + 2) + t + 2)
                            for half in range(2):
                                for j in range(T):
                                    last = nc.tensor.matmul(
                                        ps_gat[:, half, :], valid_t[:, j * N + t * P:j * N + (t + 1) * P],
                                        one_hot[1][:, j * N + half * HALF:j * N + (half + 1) * HALF],
                                        start=(j == 0), stop=(j == T - 1))
                            last.then_inc(slow_to_v, 1)
                        pe.wait_ge(slow_to_pe, c * (T + 2) + T + 2)
                    pe.sem_clear(slow_to_pe)
                    pe.drain().then_inc(slow_to_v, 1)

            graph(0)
            if B > 1:
                with pe.Fori(1, B) as g:
                    graph(g)

        @block.vector
        def _(dve):
            v = nc.vector
            st = Steps(dve, v_step)
            dve.wait_ge(const_pool, 1)
            dve.wait_ge(const_in, 160)
            dve.wait_ge(misc_read_act, 2)

            def slow_v(g):
                settle(dve)
                many = dve.value_load(flag[0:1, 0:1], min_val=0, max_val=1)
                with dve.If(many > 0):
                    ss = Steps(dve, slow_step)

                    def step(ins):
                        ss.done(ins)
                        ss.wait()

                    spread, masked = slots[:, 0:N], slots[:, N:2 * N]
                    step(v.tensor_scalar(valid_t[:, :], pos_t[:, :], 1.0, None, ALU.is_ge))
                    for t in range(T):
                        block_t = valid_t[:, t * DIAG:t * DIAG + P]
                        step(v.tensor_tensor(block_t, block_t, ident_b[:, :], ALU.add))
                    step(v.tensor_scalar(q_hi[:, :, :], q_pos[:, :, :], 1.0, None, ALU.add))
                    step(v.tensor_scalar(q_frac[:, :, :], q_pos[:, :, :], 0.375, None, ALU.subtract))
                    step(v.tensor_scalar(q_frac[:, :, :], q_frac[:, :, :], ROUND, ROUND, ALU.add, ALU.subtract))
                    step(v.tensor_tensor(q_frac[:, :, :], q_pos[:, :, :], q_frac[:, :, :], ALU.subtract))
                    ss.restart()
                    h_by_col = h[:, :].rearrange("p (t c) -> p c t", t=T)
                    agg_by_col = agg[:, :].rearrange("p (t c) -> p c t", t=T)
                    with dve.Fori(0, C) as c:
                        step(v.tensor_copy(col[:, :], h_by_col[:, c, :]))
                        dve.sem_inc(slow_to_pe, 1)
                        dve.wait_ge(slow_to_v, c * (T + 1) + 1)
                        step(v.tensor_copy(spread.rearrange("p (a n) -> p a n", a=2), ps_gat[:, :, :]))
                        for j in range(T):
                            step(v.tensor_scalar(one_hot[1][:, j * N:(j + 1) * N], spread, col[:, j:j + 1], None,
                                                 ALU.is_gt))
                        dve.sem_inc(slow_to_pe, 1)
                        for t in range(T):
                            dve.wait_ge(slow_to_v, c * (T + 1) + 2 + t)
                            for q in range(3):
                                for hi, (bound, op) in enumerate(((q_pos, ALU.is_le), (q_hi, ALU.is_lt))):
                                    step(v.scalar_tensor_tensor(
                                        masked.rearrange("p (a n) -> p a n", a=2), ps_gat[:, :, :],
                                        bound[:, q, t:t + 1], spread.rearrange("p (a n) -> p a n", a=2), op, ALU.mult))
                                    step(v.tensor_reduce(q_val[:, hi, q:q + 1], masked, AX.X, ALU.max))
                            dve.sem_inc(slow_to_pe, 1)
                            step(v.tensor_tensor(q_val[:, 1, :], q_val[:, 1, :], q_val[:, 0, :], ALU.subtract))
                            step(v.tensor_tensor(q_val[:, 1, :], q_val[:, 1, :], q_frac[:, :, t], ALU.mult))
                            step(v.tensor_tensor(q_val[:, 0, :], q_val[:, 1, :], q_val[:, 0, :], ALU.add))
                            step(v.tensor_tensor(q_val[:, 0, :], q_val[:, 0, :], quant_w[:, :], ALU.mult))
                            step(v.tensor_reduce(col_agg[:, t:t + 1], q_val[:, 0, :], AX.X, ALU.add))
                        step(v.tensor_copy(agg_by_col[:, c, :], col_agg[:, :]))
                        ss.restart()
                    dve.wait_ge(slow_to_v, C * (T + 1) + 1)
                    dve.sem_clear(slow_to_v)

            def graph(g):
                mark_at, prods = [0], [0]

                def step(ins):
                    st.done(ins)
                    st.wait()

                def mark(name):
                    mark_at[0] += 1
                    assert V[name] == mark_at[0], name
                    dve.sem_inc(v_mark, 1)

                def tell(s):
                    dve.sem_inc(s, 1)

                def layer_norm(i, after_std):
                    step(v.tensor_reduce(s_sum, tiles(x), AX.X, ALU.add))
                    step(v.scalar_tensor_tensor(tiles(xc), over_c(s_sum), -1.0 / C, tiles(x), ALU.mult, ALU.add))
                    step(v.tensor_tensor(sq[:, :], xc[:, :], xc[:, :], ALU.mult))
                    step(v.tensor_reduce(s_var, tiles(sq), AX.X, ALU.add))
                    tell(var_ready)
                    dve.wait_ge(std_ready, g * 4 + i + 1)
                    step(v.reciprocal(s_rstd, s_std))
                    step(v.scalar_tensor_tensor(tiles(h), tiles(xc), 0.0, over_c(s_rstd), ALU.max, ALU.mult))

                def split(i, src):
                    tell(y_ready)
                    dve.wait_ge(hi_ready, g * 6 + i + 1)
                    step(v.tensor_tensor(tiles(res), tiles(src), parts[:, :, 0:C], ALU.subtract))
                    tell(res_ready)
                    dve.wait_ge(mid_ready, g * 6 + i + 1)
                    step(v.tensor_tensor(parts[:, :, 2 * C:3 * C], tiles(res), parts[:, :, C:2 * C], ALU.subtract))

                def prod_done():
                    prods[0] += 1
                    n = prods[0]
                    dve.wait_ge(prod_full, g * PROD + n)

                def rows(a, t):
                    return a[:, t * N:(t + 1) * N]

                dve.wait_ge(x_loaded, (g + 1) * 16)
                layer_norm(0, None)
                mark("h0")
                dve.wait_ge(root_ready, g + 1)
                step(v.reciprocal(d0, root))
                step(v.tensor_scalar(root, root, 1e-7, None, ALU.add))
                step(v.reciprocal(d1, root))
                dve.wait_ge(misc_full, g * MISC + 1)
                step(v.tensor_tensor(tiles(y), ps_misc[:, :].rearrange("p (t c) -> p t c", t=T), over_c(d0), ALU.mult))
                split(0, y)
                mark("parts0")

                dve.wait_ge(thresholds_ready, g + 1)
                for t in range(T):
                    step(v.tensor_tensor(rows(cum, t), rows(cum, t), rows(adj_n, t), ALU.mult))
                    step(v.tensor_scalar(rows(keep, t), rows(cum, t), m_drop1[:, t:t + 1], None, ALU.not_equal))
                    step(v.scalar_tensor_tensor(rows(keep, t), rows(cum, t), m_drop2[:, t:t + 1], rows(keep, t),
                                                ALU.not_equal, ALU.mult))
                    step(v.tensor_tensor(rows(cum, t), rows(cum, t), rows(keep, t), ALU.mult))
                    mark(f"pos{t}")

                prod_done()
                step(v.tensor_tensor(y[:, :], y[:, :], ps_prod[:, :], ALU.add))
                mark("prod0_read")
                step(v.scalar_tensor_tensor(tiles(y), tiles(y), 0.0, over_c(d0), ALU.max, ALU.mult))
                step(v.tensor_tensor(x[:, :], x[:, :], y[:, :], ALU.add))

                layer_norm(1, None)
                mark("h1")
                dve.wait_ge(misc_read_act, 2 + g * MISC_ACT + T // 2)
                for i in (1, 2, 3):
                    src = g_l1[:, :, DEPTH * C:(DEPTH + 1) * C] if i == 1 else tiles(y)
                    step(v.tensor_tensor(tiles(y), src, over_c(d1), ALU.mult))
                    split(i, y)
                    mark(f"parts{i}")
                    if i == 1:
                        for t in range(T):
                            if t == 0:
                                dve.wait_ge(tr_free, g * TR + 2 * T + 2)
                            step(v.tensor_tensor(rows(pos_t, t), rows(pos_t, t), rows(keep, t), ALU.mult))
                    prod_done()
                    step(v.tensor_tensor(y[:, :], y[:, :], ps_prod[:, :], ALU.add))
                    mark(f"prod{i}_read")
                    step(v.tensor_tensor(tiles(y), tiles(y), over_c(d1), ALU.mult))
                    step(v.tensor_tensor(tiles(y), tiles(y), g_l1[:, :, (DEPTH - i) * C:(DEPTH - i + 1) * C], ALU.add))
                step(v.tensor_tensor(x[:, :], x[:, :], y[:, :], ALU.add))
                step(v.tensor_tensor(tiles(x), tiles(x), over_t(bias_l1[:, :]), ALU.add))

                layer_norm(2, None)
                mark("h2")
                split(4, h)
                mark("parts_h2")
                step(v.tensor_scalar(valid_t[:, :], pos_t[:, :], 1.0, None, ALU.is_ge))
                mark("valid")
                for k in range(1, SLOTS):
                    if k == 2:
                        dve.wait_ge(gat_full, g * GAT + 1)
                    elif k > 2:
                        dve.wait_ge(gat_full, g * GAT + k - 1)
                    step(v.tensor_scalar(one_hot[k % 2][:, :], pos_t[:, :], float(k), None, ALU.is_equal))
                    mark(f"hot{k}")
                dve.wait_ge(gat_free, (g + 1) * GAT)
                wire = {0: h} | {k: slot[k - 1] for k in range(1, SLOTS)}
                spare = slot[SLOTS - 1:]
                TOP = int(0.75 * (SLOTS - 1)) + 1
                for layer in pruned(NETWORK, [SLOTS - 1 - r for r in range(TOP + 1)]):
                    st.wait()
                    for i, (a, b, low, high) in enumerate(layer):
                        if i:
                            st.wait(2)
                        ins = (wire[a], wire[b])
                        if low:
                            wire[a] = spare.pop(0)
                            st.done(v.tensor_tensor(wire[a][:, :], ins[0][:, :], ins[1][:, :], ALU.min))
                        if high:
                            wire[b] = spare.pop(0)
                            st.done(v.tensor_tensor(wire[b][:, :], ins[0][:, :], ins[1][:, :], ALU.max))
                        spare += [w for w in ins if w is not h]
                st.wait()
                dve.wait_ge(weights_ready, g + 1)
                for r in range(TOP + 1):
                    s = wire[SLOTS - 1 - r]
                    w = over_c(w_rank[:, :, r])
                    if r == 0:
                        step(v.tensor_tensor(tiles(agg), tiles(s), w, ALU.mult))
                    else:
                        step(v.tensor_tensor(tiles(s), tiles(s), w, ALU.mult))
                        step(v.tensor_tensor(agg[:, :], agg[:, :], s[:, :], ALU.add))
                slow_v(g)
                mark("sorted")
                step(v.tensor_tensor(agg[:, :], agg[:, :], h[:, :], ALU.add))
                mark("mlp_in")
                dve.wait_ge(misc_full, g * MISC + 1 + T // 2 + 3)
                step(v.tensor_tensor(tiles(y), ps_misc[:, :].rearrange("p (t c) -> p t c", t=T),
                                     over_t(bias_l2[:, :]), ALU.add))
                mark("y_read")
                step(v.tensor_tensor(tiles(y), tiles(y), over_c(mask_g[:, :]), ALU.mult))
                step(v.tensor_tensor(x[:, :], x[:, :], y[:, :], ALU.add))

                layer_norm(3, None)
                mark("h3")
                dve.wait_ge(misc_full, (g + 1) * MISC)
                step(v.tensor_copy(y[:, :], ps_misc[:, :]))
                mark("w3_read")
                split(5, y)
                mark("parts_l3")
                step(v.tensor_tensor(tiles(x), tiles(x), over_t(bias_l3[:, :]), ALU.add))
                prod_done()
                step(v.tensor_tensor(x[:, :], x[:, :], ps_prod[:, :], ALU.add))
                mark("prod_l3_read")
                mark("result")
                assert mark_at[0] == VM
                st.restart()

            graph(0)
            if B > 1:
                with dve.Fori(1, B) as g:
                    graph(g)


_INS = ["x", "adj", "nodemask", "L0_gnn_kernel", "L1_gnn_W", "L1_gnn_b", "L2_gnn_W1", "L2_gnn_b1", "L2_gnn_W2",
        "L2_gnn_b2", "L3_gnn_weight", "L3_gnn_bias"]


def kernel(**inputs):
    import numpy as _np
    import concourse.bacc as _bacc
    from concourse import mybir as _mybir
    from concourse.bass_utils import run_bass_kernel_spmd as _run

    nc = _bacc.Bacc("TRN2", target_bir_lowering=False, num_devices=1)
    arrays, args = {}, []
    for name in _INS:
        a = _np.ascontiguousarray(inputs[name])
        if a.dtype == _np.bool_:
            a = a.view(_np.uint8)
        arrays[f"in_{name}"] = a
        args.append(nc.dram_tensor(f"in_{name}", a.shape, _mybir.dt.from_np(a.dtype), kind="ExternalInput").ap())
    shape = inputs["x"].shape
    out = nc.dram_tensor("out", shape, _mybir.dt.float32, kind="ExternalOutput").ap()
    gnn_stack(nc, *args, out)
    r = _run(nc, [arrays], core_ids=[0])
    return r.results[0]["out"]
```

```python
from contextlib import ExitStack

import concourse.bass as bass
from concourse import mybir

NETWORK_8 = [
    [(0, 2), (1, 3), (4, 6), (5, 7)],
    [(0, 4), (1, 5), (2, 6), (3, 7)],
    [(0, 1), (2, 3), (4, 5), (6, 7)],
    [(2, 4), (3, 5)],
    [(1, 4), (3, 6)],
    [(1, 2), (3, 4), (5, 6)],
]
NETWORK_16 = [
    [(i, i + 1) for i in range(0, 16, 2)],
    [(0, 2), (4, 6), (8, 10), (12, 14), (1, 3), (5, 7), (9, 11), (13, 15)],
    [(0, 4), (8, 12), (1, 5), (9, 13), (2, 6), (10, 14), (3, 7), (11, 15)],
    [(i, i + 8) for i in range(8)],
    [(5, 10), (6, 9), (3, 12), (13, 14), (7, 11), (1, 2), (4, 8)],
    [(1, 4), (7, 13), (2, 8), (11, 14)],
    [(2, 4), (5, 6), (9, 10), (11, 13), (3, 8), (7, 12)],
    [(6, 8), (10, 12), (3, 5), (7, 9)],
    [(3, 4), (5, 6), (7, 8), (9, 10), (11, 12)],
    [(6, 7), (8, 9)],
]
SLOTS = 8
WIDE = 16
T_THRESH = 10
ROUND = 8388608.0


def pruned(network, wanted):
    live, out = set(wanted), []
    for layer in reversed(network):
        out.append([(a, b, a in live, b in live) for a, b in layer if a in live or b in live])
        live |= {i for a, b, _, _ in out[-1] for i in (a, b)}
    return out[::-1]


class Steps:

    def __init__(self, engine, sem):
        self.engine, self.sem, self.n = engine, sem, 0

    def restart(self):
        self.wait()
        self.engine.sem_clear(self.sem)
        self.n = 0

    def done(self, ins):
        ins.then_inc(self.sem, 1)
        self.n += 1

    def wait(self, lag=0):
        if self.n > lag:
            self.engine.wait_ge(self.sem, self.n - lag)


def at_least(engine, sem, value):
    if isinstance(value, int) and value <= 0:
        return
    engine.wait_ge(sem, value)


def gnn_stack(nc, x_in, adj, nodemask, w_l0, w_l1, b_l1, w1, b1, w2, b2, w_l3, b_l3, out, limit=WIDE - 1):
    f32, bf16, f16 = mybir.dt.float32, mybir.dt.bfloat16, mybir.dt.float16
    i32, u8 = mybir.dt.int32, mybir.dt.uint8
    ALU, ACT, AX = mybir.AluOpType, mybir.ActivationFunctionType, mybir.AxisListType

    B, N, C = x_in.shape
    P = 128
    T = N // P
    H = w1.shape[1]
    HALF = N // 2
    F = T * C
    DEPTH = 3
    EPS = 1e-5
    RING = 2
    DIAG = N + P

    x_v = x_in.rearrange("b (t p) c -> b p t c", p=P)
    out_v = out.rearrange("b (t p) c -> b p t c", p=P)
    adj_v = adj.rearrange("b (t p) m -> b t p m", p=P)

    ctx = ExitStack()
    with ctx:
        def sb(name, shape, dt):
            return ctx.enter_context(nc.sbuf_tensor(name, shape, dt))

        def pb(name, shape, dt):
            return ctx.enter_context(nc.psum_tensor(name, shape, dt))

        def sem(name):
            return ctx.enter_context(nc.semaphore(name))

        ident_f = sb("ident_f", [P, P], f32)
        ident_b = sb("ident_b", [P, P], bf16)
        ident_h = sb("ident_h", [P, P], f16)
        off_diag = sb("off_diag", [P, P], bf16)
        prefix = sb("prefix", [P, N], bf16)
        ones_col = sb("ones_col", [P, 1], bf16)
        ones = sb("ones", [P, P], bf16)
        ranks = sb("ranks", [P, WIDE], f32)
        places = sb("places", [P, P], f16)
        quant_w = sb("quant_w", [P, 3], f32)
        eps_col = sb("eps_col", [P, 1], f32)
        w_l0_sb = sb("w_l0_sb", [C, C], f32)
        w_l1_sb = sb("w_l1_sb", [C, (DEPTH + 1) * C], f32)
        w1_sb = sb("w1_sb", [C, H], f32)
        b1_sb = sb("b1_sb", [H, 1], f32)
        w2_sb = sb("w2_sb", [H, C], f32)
        w_l3_sb = sb("w_l3_sb", [C, C], f32)
        bias_l1 = sb("bias_l1", [P, C], f32)
        bias_l2 = sb("bias_l2", [P, C], f32)
        bias_l3 = sb("bias_l3", [P, C], f32)
        mask_raw = sb("mask_raw", [B * T, P], u8)
        mask = sb("mask", [P, B, T], f32)
        mask_x = sb("mask_x", [P, T], f32)
        mask_y = sb("mask_y", [P, T], f32)

        adj_f = sb("adj_f", [P, RING, N], f32)
        adj_n = sb("adj_n", [P, T * N], f16)
        cum = adj_n
        adj_t = [sb(f"adj_t{i}", [P, T * N], bf16) for i in range(2)]
        nbr_diag = sb("nbr_diag", [P, T, P], bf16)
        keep = sb("keep", [P, T * N], f16)
        pos_t = sb("pos_t", [P, T * N], f16)
        one_hot = [sb(f"one_hot{i}", [P, T * N], bf16) for i in range(2)]
        valid_t = one_hot[0]
        keep_t = one_hot[0]
        wide = sb("wide", [P, T], bf16)
        place = sb("place", [P, T], f32)
        select = [sb(f"select{i}", [P, T, P], bf16) for i in range(2)]
        select_t = [sb(f"select_t{i}", [P, N], bf16) for i in range(2)]
        pos_w = sb("pos_w", [P, T * P], f16)
        slots_w = sb("slots_w", [P, 2 * WIDE * C], f32)
        agg_w = sb("agg_w", [P, C], f32)
        rest_w = sb("rest_w", [P, C], f32)
        parts_w = sb("parts_w", [P, 3 * C], bf16)
        cnt_b = sb("cnt_b", [P, T], bf16)
        cnt_w = sb("cnt_w", [P, 1], f32)
        w_rank_w = sb("w_rank_w", [P, WIDE], f32)

        x = [sb(f"x{i}", [P, F], f32) for i in range(2)]
        h = sb("h", [P, F], f32)
        h2 = sb("h2", [P, F], f32)
        y = sb("y", [P, F], f32)
        z = sb("z", [P, F], f32)
        res = sb("res", [P, F], f32)
        mask_rows = res[0:B * T, 0:P]
        xc = res
        parts_h2 = sb("parts_h2", [P, T, 3 * C], bf16)
        parts = sb("parts", [P, T, 3 * C], bf16)
        h_t = sb("h_t", [C, N], f32)
        g_l1 = sb("g_l1", [P, T, (DEPTH + 1) * C], f32)
        w_l1_rows = y[0:C, 0:(DEPTH + 1) * C]
        slots = sb("slots", [P, (SLOTS + 4) * F], f32)
        slot = [slots[:, i * F:(i + 1) * F] for i in range(SLOTS + 4)]
        hid_t = slots[0:H, 0:N]
        agg = z
        stat = sb("stat", [P, 8, T], f32)
        deg, d0, d1, s_sum, s_var, s_std, s_rstd, root = [stat[:, i, :] for i in range(8)]
        dil = sb("dil", [P, 6, T], f32)
        m_all, m_skip, m_do, m_drop1, m_drop2, m_cnt = [dil[:, i, :] for i in range(6)]
        m_max = sb("m_max", [P, 2 * T], f32)[:, :]
        q_pos_w = sb("q_pos_w", [P, 3], f32)
        narrow = sb("narrow", [P, T], f32)
        over = sb("over", [P, 2, T], f32)
        flag = sb("flag", [P, 1], i32)
        q_pos = sb("q_pos", [P, 3, T], f32)
        hat = sb("hat", [P, 2, 3 * T * SLOTS], f32)
        w_rank = sb("w_rank", [P, T, SLOTS], f32)

        q_hi = sb("q_hi", [P, 3, T], f32)
        q_frac = sb("q_frac", [P, 3, T], f32)
        col = sb("col", [P, T], f32)
        col_agg = sb("col_agg", [P, T], f32)
        q_val = sb("q_val", [P, 2, 3], f32)

        ps_tr = [pb(f"ps_tr{i}", [P, HALF], f32) for i in range(2)]
        ps_cum = pb("ps_cum", [P, N], f32)
        ps_prod = pb("ps_prod", [P, F], f32)
        ps_gat = pb("ps_gat", [P, 2, HALF], f32)
        ps_misc = pb("ps_misc", [P, HALF], f32)

        const_in = sem("const_in")
        const_pool = sem("const_pool")
        const_pe = sem("const_pe")
        const_v = sem("const_v")
        x_loaded = sem("x_loaded")
        adj_loaded = [sem(f"adj_loaded{i}") for i in range(RING)]
        cast_done = sem("cast_done")
        tr_full, tr_free = sem("tr_full"), sem("tr_free")
        cum_full, cum_read_v, cum_read_act = sem("cum_full"), sem("cum_read_v"), sem("cum_read_act")
        prod_x, prod_y = sem("prod_x"), sem("prod_y")
        gat_full, gat_free = sem("gat_full"), sem("gat_free")
        const_act = sem("const_act")
        misc_x, misc_x_act = sem("misc_x"), sem("misc_x_act")
        misc_y, misc_y_act = sem("misc_y"), sem("misc_y_act")
        nbr_ready = sem("nbr_ready")
        wide_ready = sem("wide_ready")
        cnt_ready = sem("cnt_ready")
        thresholds_ready = sem("thresholds_ready")
        tables_ready, weights_ready, weights_w_ready = [sem(n) for n in ("tables_ready", "weights_ready",
                                                                         "weights_w_ready")]
        var, std, src_ready, hi_ready, rest_ready, mid_ready = [
            [sem(f"{n}_{half}") for half in "xy"] for n in ("var", "std", "src", "hi", "rest", "mid")]
        root_ready = sem("root_ready")
        slow_to_pe, slow_to_v = sem("slow_to_pe"), sem("slow_to_v")
        v_step, pool_step = sem("v_step"), sem("pool_step")
        x_mark, y_mark = sem("x_mark"), sem("y_mark")
        slow_step = sem("slow_step")
        out_done = sem("out_done")
        settled = sem("settled")

        def tiles(a):
            return a[:, :].rearrange("p (t c) -> p t c", t=T)

        def over_c(s):
            return s.unsqueeze(2).to_broadcast([P, T, C])

        def over_t(row):
            return row.unsqueeze(1).to_broadcast([P, T, C])

        TR_X = 3 * T + 4
        TR = TR_X + 4
        CUM = T + 2
        GAT = SLOTS + 2
        MISC_X = 2 + T // 2
        MISC_Y = 6

        X_MARKS = (["h0", "parts0", "select"] + [f"keep{t}" for t in range(T)] + ["h1", "parts1"]
                   + [f"pos{t}" for t in range(T)] + ["parts2", "parts3", "parts_h2"])
        Y_MARKS = (["valid"] + [f"hot{k}" for k in range(1, SLOTS)]
                   + ["hot_w_low", "hot_w_high", "slow_done", "sorted_w", "mlp_in", "y_read", "h3", "parts_l3",
                      "result"])

        def x_reached(engine, g, name):
            engine.wait_ge(x_mark, g * len(X_MARKS) + X_MARKS.index(name) + 1)

        def y_reached(engine, g, name):
            engine.wait_ge(y_mark, g * len(Y_MARKS) + Y_MARKS.index(name) + 1)

        def run(engine, stretch):
            stretch(None, 0, 0)
            if B > 2:
                with engine.Fori(0, (B - 2) // 2) as i:
                    stretch(i * 2, i * 2 + 1, 1)
                    stretch(i * 2 + 1, i * 2 + 2, 0)
            stretch(B - 2, B - 1, 1)
            stretch(B - 1, None, 0)

        def hot_w(k):
            return one_hot[k // SLOTS][:, k % SLOTS * N:(k % SLOTS + 1) * N]

        def settle(engine):
            engine.sem_inc(settled, 1)

        block = ctx.enter_context(nc.Block())

        @block.sync
        def _(sp):
            for dst, src in [(w_l0_sb[:, :], w_l0), (w_l1_rows[:, :], w_l1), (w1_sb[:, :], w1),
                             (b1_sb[:, :], b1.unsqueeze(1)), (w2_sb[:, :], w2), (w_l3_sb[:, :], w_l3),
                             (bias_l1[:, :], b_l1.partition_broadcast(P)), (bias_l2[:, :], b2.partition_broadcast(P)),
                             (bias_l3[:, :], b_l3.partition_broadcast(P)),
                             (mask_raw[:, :], nodemask.rearrange("b (t p) -> (b t) p", p=P))]:
                sp.dma_start(dst, src).then_inc(const_in, 16)

            def load(g, par):
                sp.dma_start(tiles(x[par]), x_v[g]).then_inc(x_loaded, 16)
                for t in range(T):
                    at_least(sp, cast_done, g * T + (t + 1 - RING))
                    settle(sp)
                    sp.dma_start(adj_f[:, t % RING, :], adj_v[g, t]).then_inc(adj_loaded[t % RING], 16)

            def stretch(a, b, par):
                if b is not None:
                    load(b, par)
                if a is not None:
                    y_reached(sp, a, "result")
                    settle(sp)
                    sp.dma_start(out_v[a], tiles(x[1 - par])).then_inc(out_done, 16)
                    if not (isinstance(a, int) and a == B - 1):
                        sp.wait_ge(out_done, (a + 1) * 16)
                        settle(sp)

            run(sp, stretch)
            sp.wait_ge(out_done, 16 * B)

        @block.gpsimd
        def _(pool):
            st = Steps(pool, pool_step)

            def step(ins):
                st.done(ins)
                st.wait()

            for m in (ident_f, ident_b, ident_h):
                step(pool.memset(m[:, :], 0.0))
                step(pool.affine_select(out=m[:, :], in_=m[:, :], compare_op=ALU.not_equal, fill=1.0, base=0,
                                        pattern=[[-1, P]], channel_multiplier=1))
            step(pool.memset(off_diag[:, :], 1.0))
            step(pool.affine_select(out=off_diag[:, :], in_=off_diag[:, :], compare_op=ALU.not_equal, fill=0.0,
                                    base=0, pattern=[[-1, P]], channel_multiplier=1))
            step(pool.memset(prefix[:, :], 1.0))
            step(pool.affine_select(out=prefix[:, 0:P], in_=prefix[:, 0:P], compare_op=ALU.is_ge, fill=0.0, base=0,
                                    pattern=[[1, P]], channel_multiplier=-1))
            step(pool.memset(ones_col[:, :], 1.0))
            step(pool.memset(eps_col[:, :], EPS))
            step(pool.memset(ones[:, :], 1.0))
            step(pool.iota(places[:, :], [[1, P]], base=1, channel_multiplier=0,
                           allow_small_or_imprecise_dtypes=True))
            for r in range(WIDE):
                step(pool.memset(ranks[:, r:r + 1], float(r)))
            for q, w in enumerate((0.25, 0.5, 0.25)):
                step(pool.memset(quant_w[:, q:q + 1], w))
            pool.wait_ge(const_in, 160)
            step(pool.tensor_copy(mask_rows[:, :], mask_raw[:, :]))
            pool.sem_inc(const_pool, 1)

            def diagonals(dst, src, factor, op):
                rows = src[:, 0:(T - 1) * DIAG].rearrange("p (t s) -> p t s", s=DIAG)[:, :, 0:P]
                to = dst[0] if isinstance(dst, tuple) else dst[:, 0:(T - 1) * DIAG].rearrange(
                    "p (t s) -> p t s", s=DIAG)[:, :, 0:P]
                last = dst[1] if isinstance(dst, tuple) else dst[:, (T - 1) * DIAG:T * N]
                st.done(pool.tensor_tensor(to, rows, factor[:, :].unsqueeze(1).to_broadcast([P, T - 1, P]), op))
                st.done(pool.tensor_tensor(last, src[:, (T - 1) * DIAG:T * N], factor[:, :], op))

            def rank_weights(out, groups, n_ranks, positions):
                size = 3 * groups * n_ranks
                a, c = [hat[:, i, 0:size].rearrange("p (t r) -> p t r", r=n_ranks) for i in range(2)]
                step(pool.tensor_tensor(a, ranks[:, 0:n_ranks].unsqueeze(1).to_broadcast([P, 3 * groups, n_ranks]),
                                        positions.unsqueeze(2).to_broadcast([P, 3 * groups, n_ranks]), ALU.subtract))
                step(pool.tensor_scalar(c, a, 0.0, None, ALU.max))
                step(pool.tensor_scalar(a, a, 0.0, None, ALU.min))
                step(pool.tensor_tensor(a, a, c, ALU.subtract))
                step(pool.tensor_scalar(a, a, 1.0, None, ALU.add))
                step(pool.tensor_scalar(a, a, 0.0, 0.25, ALU.max, ALU.mult))
                q = hat[:, 0, 0:size].rearrange("p (q t r) -> p q t r", q=3, r=n_ranks)
                step(pool.tensor_tensor(out, q[:, 0], q[:, 2], ALU.add))
                step(pool.tensor_tensor(out, out, q[:, 1], ALU.add))
                step(pool.tensor_tensor(out, out, q[:, 1], ALU.add))

            def first_half(g, par):
                pool.wait_ge(tr_full, g * TR + T)
                diagonals(adj_n, adj_n, off_diag, ALU.mult)
                pool.wait_ge(tr_free, g * TR + T)
                diagonals((nbr_diag[:, 0:T - 1, :], nbr_diag[:, T - 1, :]), adj_t[par], off_diag, ALU.mult)
                st.wait()
                pool.sem_inc(nbr_ready, 1)

                pool.wait_ge(cum_read_v, 2 * (g + 1) * T)
                settle(pool)
                step(pool.tensor_scalar(wide[:, :], m_all, float(SLOTS - 1), None, ALU.is_gt))
                pool.sem_inc(wide_ready, 1)
                step(pool.tensor_copy(mask_x[:, :], mask[:, g, :]))
                step(pool.tensor_scalar(m_skip, m_all, 0.5, 0.25, ALU.mult, ALU.add))
                step(pool.tensor_scalar(m_skip, m_skip, ROUND, ROUND, ALU.add, ALU.subtract))
                step(pool.tensor_scalar(m_do, m_all, float(T_THRESH), None, ALU.is_gt))
                step(pool.tensor_tensor(m_do, m_do, mask_x[:, :], ALU.mult))
                step(pool.tensor_tensor(m_skip, m_skip, m_do, ALU.mult))
                step(pool.tensor_tensor(m_skip, m_skip, m_do, ALU.add))
                step(pool.tensor_scalar(m_drop1, m_skip, -1.0, None, ALU.add))
                step(pool.tensor_scalar(m_drop2, m_drop1, 2.0, None, ALU.mult))
                pool.sem_inc(thresholds_ready, 1)
            def second_half_narrow(g):
                pool.wait_ge(gat_free, g * GAT + 1)
                settle(pool)
                step(pool.tensor_copy(cnt_b[:, :], m_cnt))
                pool.sem_inc(cnt_ready, 1)
                step(pool.tensor_copy(mask_y[:, :], mask[:, g, :]))
                step(pool.tensor_scalar(narrow[:, :], m_all, float(SLOTS - 1), None, ALU.is_le))
                step(pool.tensor_scalar(m_max[:, 0:T], m_all, float(limit), None, ALU.is_gt))
                step(pool.tensor_scalar(m_max[:, T:2 * T], narrow[:, :], -1.0, 1.0, ALU.mult, ALU.add))
                step(pool.partition_all_reduce(over[:, :, :].rearrange("p a t -> p (a t)"), m_max, P,
                                               bass.bass_isa.ReduceOp.add))
                half = T // 2
                while half:
                    step(pool.tensor_tensor(over[:, :, 0:half], over[:, :, 0:half], over[:, :, half:2 * half],
                                            ALU.add))
                    half //= 2
                step(pool.tensor_scalar(over[:, 1, 0:1], over[:, 1, 0:1], float(P), None, ALU.is_gt))
                step(pool.tensor_tensor(over[:, 0, 0:1], over[:, 0, 0:1], over[:, 1, 0:1], ALU.add))
                step(pool.tensor_scalar(over[:, 0, 0:1], over[:, 0, 0:1], 0.0, None, ALU.is_gt))
                step(pool.tensor_copy(flag[:, :], over[:, 0, 0:1]))

                pool.sem_inc(tables_ready, 1)
                for q, tau in enumerate((0.25, 0.5, 0.75)):
                    step(pool.tensor_scalar(q_pos[:, q, :], m_cnt, tau, None, ALU.mult))
                rank_weights(w_rank[:, :, :], T, SLOTS, q_pos[:, :, :].rearrange("p q t -> p (q t)"))
                step(pool.tensor_tensor(w_rank[:, :, :], w_rank[:, :, :],
                                        narrow[:, :].unsqueeze(2).to_broadcast([P, T, SLOTS]), ALU.mult))
                pool.sem_inc(weights_ready, 1)

            def second_half_wide(g):
                pool.wait_ge(misc_y_act, g * 3 + 1)
                settle(pool)
                for q, tau in enumerate((0.25, 0.5, 0.75)):
                    step(pool.tensor_scalar(q_pos_w[:, q:q + 1], cnt_w[:, :], tau, None, ALU.mult))
                rank_weights(w_rank_w[:, :].unsqueeze(1), 1, WIDE, q_pos_w[:, :])
                pool.sem_inc(weights_w_ready, 1)

            def stretch(a, b, par):
                st.restart()
                if a is not None:
                    second_half_narrow(a)
                if b is not None:
                    first_half(b, par)
                if a is not None:
                    second_half_wide(a)

            run(pool, stretch)

        @block.scalar
        def _(act):
            act.wait_ge(const_pool, 1)
            act.wait_ge(const_pe, 2)
            act.activation(mask[:, :, :].rearrange("p b t -> p (b t)"), ps_misc[:, 0:B * T], ACT.Copy)\
               .then_inc(const_act, 1)
            act.activation(w_l1_sb[:, :], ps_prod[0:C, 0:(DEPTH + 1) * C], ACT.Copy).then_inc(const_act, 1)

            def stretch(a, b, par):
                tr_a = None if a is None else (a + 1) * TR + (0 if b is None else TR_X)

                def from_tr(n, dst, bank_view):
                    act.wait_ge(tr_full, n)
                    act.activation(dst, bank_view, ACT.Copy).then_inc(tr_free, 1)

                def from_tiles(n, dst, t):
                    bank = ps_tr[t % 2][:, :].bitcast(f16).rearrange("p (j n) -> p j n", j=T)
                    from_tr(n + t, dst[:, :].rearrange("p (j n) -> p j n", j=T)[:, :, t * P:(t + 1) * P], bank)

                def feature_rows(n):
                    for i in range(2):
                        from_tr(n + i, h_t[:, i * HALF:(i + 1) * HALF], ps_tr[i][0:C, :])

                def deviation(half, n):
                    act.wait_ge(var[half], n)
                    act.activation(s_std, s_var, ACT.Sqrt, bias=eps_col[:, :], scale=1.0 / C).then_inc(std[half], 1)

                def split(half, n, src, to):
                    act.wait_ge(src_ready[half], n)
                    act.activation(to[:, :, 0:C], tiles(src), ACT.Copy).then_inc(hi_ready[half], 1)
                    act.wait_ge(rest_ready[half], n)
                    act.activation(to[:, :, C:2 * C], tiles(res), ACT.Copy).then_inc(mid_ready[half], 1)

                def cast(t):
                    act.wait_ge(adj_loaded[t % RING], b * (T // RING * 16) + (t // RING + 1) * 16)
                    act.activation(adj_n[:, t * N:(t + 1) * N], adj_f[:, t % RING, :], ACT.Copy,
                                   accum_out=deg[:, t:t + 1]).then_inc(cast_done, 1)

                def narrow_slot(k):
                    act.wait_ge(gat_full, a * GAT + k + 1)
                    act.activation(slot[k - 1][:, :], ps_gat[:, k % 2, :], ACT.Copy).then_inc(gat_free, 1)

                if a is not None:
                    act.wait_ge(gat_full, a * GAT + 1)
                    act.activation(m_cnt, ps_gat[:, 0, 0:T], ACT.Copy).then_inc(gat_free, 1)
                if b is not None:
                    for t in range(T // 2):
                        cast(t)
                if a is not None:
                    narrow_slot(1)
                if b is not None:
                    for t in range(T // 2):
                        from_tiles(b * TR + 1, adj_t[par], t)
                    for t in range(T // 2, T):
                        cast(t)
                if a is not None:
                    narrow_slot(2)
                if b is not None:
                    for t in range(T // 2, T):
                        from_tiles(b * TR + 1, adj_t[par], t)
                    act.wait_ge(cast_done, (b + 1) * T)
                    act.activation(root, deg, ACT.Sqrt, bias=1.0).then_inc(root_ready, 1)
                    deviation(0, b * 3 + 1)
                    feature_rows(b * TR + T + 1)
                if a is not None:
                    narrow_slot(3)
                if b is not None:
                    split(0, b * 5 + 1, y, parts)
                if a is not None:
                    for k in range(4, SLOTS):
                        narrow_slot(k)
                    for i in range(2):
                        act.wait_ge(gat_full, a * GAT + SLOTS + i + 1)
                        act.activation(slots_w[:, i * HALF:(i + 1) * HALF], ps_gat[:, i, :], ACT.Copy)\
                           .then_inc(gat_free, 1)
                    act.wait_ge(misc_y, a * MISC_Y + 1)
                    act.activation(cnt_w[:, :], ps_misc[:, 0:1], ACT.Copy).then_inc(misc_y_act, 1)
                if b is not None:
                    deviation(0, b * 3 + 2)
                    if a is not None:
                        y_reached(act, a, "slow_done")
                    for t in range(T):
                        from_tiles(b * TR + T + 3, keep_t, t)
                    act.wait_ge(cum_full, b * CUM + T + 1)
                    act.activation(select_t[par][:, :], ps_cum[:, 0:HALF].bitcast(bf16), ACT.Copy)\
                       .then_inc(cum_read_act, 1)
                    feature_rows(b * TR + 2 * T + 3)
                    for i in range(T // 2):
                        act.wait_ge(misc_x, b * MISC_X + 3 + i)
                        act.activation(g_l1[:, 2 * i:2 * i + 2, :],
                                       ps_misc[:, :].rearrange("p (t c) -> p t c", t=2), ACT.Copy)\
                           .then_inc(misc_x_act, 1)
                    split(0, b * 5 + 2, y, parts)
                    for t in range(T // 2):
                        from_tiles(b * TR + 2 * T + 5, pos_t, t)
                    split(0, b * 5 + 3, y, parts)
                    for t in range(T // 2, T):
                        from_tiles(b * TR + 2 * T + 5, pos_t, t)
                    act.wait_ge(cum_full, (b + 1) * CUM)
                    act.activation(pos_w[:, :], ps_cum[:, :], ACT.Copy).then_inc(cum_read_act, 1)
                    split(0, b * 5 + 4, y, parts)
                if a is not None:
                    feature_rows(tr_a + 1)
                if b is not None:
                    deviation(0, b * 3 + 3)
                if a is not None:
                    for i in range(2):
                        act.wait_ge(misc_y, a * MISC_Y + 3 + i)
                        act.activation(hid_t[:, i * HALF:(i + 1) * HALF], ps_misc[:, :], ACT.Relu,
                                       bias=b1_sb[:, :]).then_inc(misc_y_act, 1)
                if b is not None:
                    split(0, b * 5 + 5, h2, parts_h2)
                if a is not None:
                    deviation(1, a + 1)
                    feature_rows(tr_a + 3)
                    split(1, a + 1, z, parts)
                else:
                    act.wait_ge(tr_free, TR_X)
                    act.sem_inc(tr_free, TR - TR_X)

            run(act, stretch)

        @block.tensor
        def _(pe):
            pe.wait_ge(const_pool, 1)
            nc.tensor.transpose(ps_misc[:, 0:B * T], mask_rows[:, :], ident_f[0:B * T, 0:B * T]).then_inc(const_pe, 1)
            for i in range(DEPTH + 1):
                last = nc.tensor.transpose(ps_prod[0:C, i * C:(i + 1) * C], w_l1_rows[:, i * C:(i + 1) * C],
                                           ident_f[0:C, 0:C])
            last.then_inc(const_pe, 1)
            pe.wait_ge(const_act, 2)

            def stretch(a, b, par):
                tr_a = None if a is None else (a + 1) * TR + (0 if b is None else TR_X)

                def transpose_tile(n, src, t):
                    at_least(pe, tr_free, n + t - 1)
                    view = ps_tr[t % 2][:, :].bitcast(f16).rearrange("p (j n) -> p j n", j=T)
                    for j in range(T):
                        last = nc.tensor.transpose(view[:, j, :], src[:, t * N + j * P:t * N + (j + 1) * P],
                                                   ident_h[:, :])
                    last.then_inc(tr_full, 1)

                def transpose_features(n, src):
                    for i in range(2):
                        pe.wait_ge(tr_free, n + i - 1)
                        settle(pe)
                        for t in range(T // 2):
                            tt = i * (T // 2) + t
                            last = nc.tensor.transpose(ps_tr[i][0:C, t * P:(t + 1) * P],
                                                       src[:, tt * C:(tt + 1) * C], ident_f[:, :])
                        last.then_inc(tr_full, 1)
                    pe.wait_ge(tr_free, n + 2)

                def product(dst, lhs_t, rhs, signal):
                    for t in range(T):
                        for j in range(T):
                            for k in range(3):
                                last = nc.tensor.matmul(dst[:, t * C:(t + 1) * C],
                                                        lhs_t[:, j * N + t * P:j * N + (t + 1) * P],
                                                        rhs[:, j, k * C:(k + 1) * C],
                                                        start=(j == 0 and k == 0), stop=(j == T - 1 and k == 2))
                    last.then_inc(signal, 1)

                def node_linear(w_sb, signal):
                    for t in range(T):
                        last = nc.tensor.matmul(ps_misc[:, t * C:(t + 1) * C], h_t[:, t * P:(t + 1) * P],
                                                w_sb[:, :], start=True, stop=True)
                    last.then_inc(signal, 1)

                def ranks_of(t):
                    at_least(pe, cum_read_v, 2 * (b * T + t))
                    at_least(pe, cum_read_act, b * 2)
                    for half in range(2):
                        lo = half * HALF
                        js = [j for j in range(T) if j * P < lo + HALF]
                        for j in js:
                            start = max(lo, j * P)
                            lhs = (nbr_diag[:, t, :] if j == t
                                   else adj_t[par][:, j * N + t * P:j * N + (t + 1) * P])
                            last = nc.tensor.matmul(ps_cum[:, start:lo + HALF], lhs,
                                                    prefix[:, start - j * P:lo + HALF - j * P],
                                                    start=(j == 0), stop=(j == js[-1]))
                    last.then_inc(cum_full, 1)

                def transpose_adjacency(t):
                    pe.wait_ge(cast_done, b * T + t + 1)
                    transpose_tile(b * TR, adj_n, t)

                def gather(k):
                    y_reached(pe, a, f"hot{k}")
                    pe.wait_ge(gat_free, a * GAT + k - 1) if k > 1 else None
                    product(ps_gat[:, k % 2, :], one_hot[k % 2], parts_h2, gat_full)

                def wide_slot(bank, at, lhs_of):
                    for j in range(T):
                        for k in range(3):
                            last = nc.tensor.matmul(ps_gat[:, bank, at * C:(at + 1) * C], lhs_of(j),
                                                    parts_h2[:, j, k * C:(k + 1) * C],
                                                    start=(j == 0 and k == 0), stop=(j == T - 1 and k == 2))
                    return last

                if a is not None:
                    y_reached(pe, a, "valid")
                    for t in range(T):
                        for j in range(T):
                            last = nc.tensor.matmul(ps_gat[:, 0, t:t + 1],
                                                    valid_t[:, j * N + t * P:j * N + (t + 1) * P],
                                                    ones_col[:, :], start=(j == 0), stop=(j == T - 1))
                    last.then_inc(gat_full, 1)
                    gather(1)
                if b is not None:
                    for t in range(T // 2):
                        transpose_adjacency(t)
                if a is not None:
                    gather(2)
                if b is not None:
                    for t in range(T // 2, T):
                        transpose_adjacency(t)
                    x_reached(pe, b, "h0")
                    transpose_features(b * TR + T, h)
                    node_linear(w_l0_sb, misc_x)
                if a is not None:
                    gather(3)
                for i in range(4):
                    if b is not None:
                        if i == 0:
                            pe.wait_ge(nbr_ready, b + 1)
                        for t in range(i * T // 4, (i + 1) * T // 4):
                            ranks_of(t)
                        if i == 3:
                            x_reached(pe, b, "parts0")
                            pe.wait_ge(wide_ready, b + 1)
                            nc.tensor.matmul(ps_misc[:, 0:T], prefix[:, 0:P], wide[:, :], start=True, stop=False)
                            for t in range(1, T):
                                last = nc.tensor.matmul(ps_misc[:, t:T], ones[:, :], wide[:, 0:T - t],
                                                        start=False, stop=(t == T - 1))
                            last.then_inc(misc_x, 1)
                    if a is not None:
                        gather(4 + i)
                if b is not None:
                    product(ps_prod, adj_t[par], parts, prod_x)
                if a is not None:
                    pe.wait_ge(gat_free, a * GAT + SLOTS - 1)
                    wide_slot(0, 0, lambda j: select[1 - par][:, j, :])
                    y_reached(pe, a, "hot_w_low")
                    for k in range(1, SLOTS):
                        last = wide_slot(0, k, lambda j: hot_w(k)[:, j * P:(j + 1) * P])
                    last.then_inc(gat_full, 1)
                    pe.wait_ge(gat_free, a * GAT + SLOTS)
                    y_reached(pe, a, "hot_w_high")
                    for k in range(SLOTS, WIDE):
                        last = wide_slot(1, k - SLOTS, lambda j: hot_w(k)[:, j * P:(j + 1) * P])
                    last.then_inc(gat_full, 1)
                    pe.wait_ge(cnt_ready, a + 1)
                    if b is not None:
                        x_reached(pe, b, "select")
                    for t in range(T):
                        last = nc.tensor.matmul(ps_misc[:, 0:1], select[1 - par][:, t, :], cnt_b[:, t:t + 1],
                                                start=(t == 0), stop=(t == T - 1))
                    last.then_inc(misc_y, 1)
                    slow_pe(pe, a)
                if b is not None:
                    for t in range(T):
                        x_reached(pe, b, f"keep{t}")
                        transpose_tile(b * TR + T + 2, keep, t)
                    pe.wait_ge(cum_read_v, 2 * (b + 1) * T)
                    for t in range(T):
                        last = nc.tensor.transpose(ps_cum[:, t * (P // 2):(t + 1) * (P // 2)].bitcast(bf16),
                                                   select[par][:, t, :], ident_b[:, :])
                    last.then_inc(cum_full, 1)
                    x_reached(pe, b, "h1")
                    transpose_features(b * TR + 2 * T + 2, h)
                    for i in range(T // 2):
                        if i:
                            pe.wait_ge(misc_x_act, b * (T // 2) + i)
                        elif a is not None:
                            pe.wait_ge(misc_y_act, a * 3 + 1)
                        for t in range(2):
                            tt = 2 * i + t
                            last = nc.tensor.matmul(ps_misc[:, t * 4 * C:(t + 1) * 4 * C],
                                                    h_t[:, tt * P:(tt + 1) * P], w_l1_sb[:, :],
                                                    start=True, stop=True)
                        last.then_inc(misc_x, 1)
                    x_reached(pe, b, "parts1")
                    product(ps_prod, adj_t[par], parts, prod_x)
                    for t in range(T):
                        x_reached(pe, b, f"pos{t}")
                        transpose_tile(b * TR + 2 * T + 4, cum, t)
                    pe.wait_ge(cum_read_act, b * 2 + 1)
                    for j in range(T):
                        for t in range(T):
                            last = nc.tensor.matmul(ps_cum[:, j * P:(j + 1) * P],
                                                    cum[:, t * N + j * P:t * N + (j + 1) * P],
                                                    select[par][:, t, :], start=(t == 0), stop=(t == T - 1))
                    last.then_inc(cum_full, 1)
                    for i in (2, 3):
                        x_reached(pe, b, f"parts{i}")
                        product(ps_prod, adj_t[par], parts, prod_x)
                if a is not None:
                    y_reached(pe, a, "sorted_w")
                    if b is not None:
                        pe.wait_ge(misc_x_act, (b + 1) * (T // 2))
                    for t in range(T):
                        for k in range(3):
                            last = nc.tensor.matmul(ps_misc[:, t * C:(t + 1) * C],
                                                    select_t[1 - par][:, t * P:(t + 1) * P],
                                                    parts_w[:, k * C:(k + 1) * C], start=(k == 0), stop=(k == 2))
                    last.then_inc(misc_y, 1)
                    y_reached(pe, a, "mlp_in")
                    transpose_features(tr_a, agg)
                    for i in range(2):
                        if i:
                            pe.wait_ge(misc_y_act, a * 3 + 2)
                        nc.tensor.matmul(ps_misc[:, :], w1_sb[:, :], h_t[:, i * HALF:(i + 1) * HALF],
                                         start=True, stop=True).then_inc(misc_y, 1)
                    pe.wait_ge(misc_y_act, (a + 1) * 3)
                    for t in range(T):
                        last = nc.tensor.matmul(ps_misc[:, t * C:(t + 1) * C], hid_t[:, t * P:(t + 1) * P],
                                                w2_sb[:, :], start=True, stop=True)
                    last.then_inc(misc_y, 1)
                    y_reached(pe, a, "h3")
                    transpose_features(tr_a + 2, h)
                    node_linear(w_l3_sb, misc_y)
                    y_reached(pe, a, "parts_l3")
                    product(ps_prod, adj_t[1 - par], parts, prod_y)
                else:
                    pe.wait_ge(tr_free, TR_X)
                    pe.sem_inc(tr_full, TR - TR_X)

            def slow_pe(pe, g):
                pe.wait_ge(tables_ready, g + 1)
                settle(pe)
                many = pe.value_load(flag[0:1, 0:1], min_val=0, max_val=1)
                with pe.If(many > 0):
                    with pe.Fori(0, C) as c:
                        pe.wait_ge(slow_to_pe, c * (T + 2) + 1)
                        for t in range(T):
                            last = nc.tensor.transpose(ps_gat[:, t // (T // 2), (t % (T // 2)) * P:(t % (T // 2) + 1) * P],
                                                       col[:, t:t + 1].to_broadcast([P, P]), ident_f[:, :])
                        last.then_inc(slow_to_v, 1)
                        for t in range(T):
                            pe.wait_ge(slow_to_pe, c * (T + 2) + t + 2)
                            for half in range(2):
                                for j in range(T):
                                    last = nc.tensor.matmul(
                                        ps_gat[:, half, :], valid_t[:, j * N + t * P:j * N + (t + 1) * P],
                                        one_hot[1][:, j * N + half * HALF:j * N + (half + 1) * HALF],
                                        start=(j == 0), stop=(j == T - 1))
                            last.then_inc(slow_to_v, 1)
                        pe.wait_ge(slow_to_pe, c * (T + 2) + T + 2)
                    pe.sem_clear(slow_to_pe)
                    pe.drain().then_inc(slow_to_v, 1)

            run(pe, stretch)

        @block.vector
        def _(dve):
            v = nc.vector
            st = Steps(dve, v_step)
            dve.wait_ge(const_pool, 1)
            dve.wait_ge(const_in, 160)
            dve.wait_ge(const_act, 2)

            def slow_v(g):
                settle(dve)
                many = dve.value_load(flag[0:1, 0:1], min_val=0, max_val=1)
                with dve.If(many > 0):
                    ss = Steps(dve, slow_step)

                    def step(ins):
                        ss.done(ins)
                        ss.wait()

                    spread, masked = slots[:, 0:N], slots[:, N:2 * N]
                    step(v.tensor_scalar(valid_t[:, :], pos_t[:, :], 1.0, None, ALU.is_ge))
                    for t in range(T):
                        block_t = valid_t[:, t * DIAG:t * DIAG + P]
                        step(v.tensor_tensor(block_t, block_t, ident_b[:, :], ALU.add))
                    step(v.tensor_scalar(q_hi[:, :, :], q_pos[:, :, :], 1.0, None, ALU.add))
                    step(v.tensor_scalar(q_frac[:, :, :], q_pos[:, :, :], 0.375, None, ALU.subtract))
                    step(v.tensor_scalar(q_frac[:, :, :], q_frac[:, :, :], ROUND, ROUND, ALU.add, ALU.subtract))
                    step(v.tensor_tensor(q_frac[:, :, :], q_pos[:, :, :], q_frac[:, :, :], ALU.subtract))
                    ss.restart()
                    h_by_col = h2[:, :].rearrange("p (t c) -> p c t", t=T)
                    agg_by_col = agg[:, :].rearrange("p (t c) -> p c t", t=T)
                    with dve.Fori(0, C) as c:
                        step(v.tensor_copy(col[:, :], h_by_col[:, c, :]))
                        dve.sem_inc(slow_to_pe, 1)
                        dve.wait_ge(slow_to_v, c * (T + 1) + 1)
                        step(v.tensor_copy(spread.rearrange("p (a n) -> p a n", a=2), ps_gat[:, :, :]))
                        for j in range(T):
                            step(v.tensor_scalar(one_hot[1][:, j * N:(j + 1) * N], spread, col[:, j:j + 1], None,
                                                 ALU.is_gt))
                        dve.sem_inc(slow_to_pe, 1)
                        for t in range(T):
                            dve.wait_ge(slow_to_v, c * (T + 1) + 2 + t)
                            for q in range(3):
                                for hi, (bound, op) in enumerate(((q_pos, ALU.is_le), (q_hi, ALU.is_lt))):
                                    step(v.scalar_tensor_tensor(
                                        masked.rearrange("p (a n) -> p a n", a=2), ps_gat[:, :, :],
                                        bound[:, q, t:t + 1], spread.rearrange("p (a n) -> p a n", a=2), op, ALU.mult))
                                    step(v.tensor_reduce(q_val[:, hi, q:q + 1], masked, AX.X, ALU.max))
                            dve.sem_inc(slow_to_pe, 1)
                            step(v.tensor_tensor(q_val[:, 1, :], q_val[:, 1, :], q_val[:, 0, :], ALU.subtract))
                            step(v.tensor_tensor(q_val[:, 1, :], q_val[:, 1, :], q_frac[:, :, t], ALU.mult))
                            step(v.tensor_tensor(q_val[:, 0, :], q_val[:, 1, :], q_val[:, 0, :], ALU.add))
                            step(v.tensor_tensor(q_val[:, 0, :], q_val[:, 0, :], quant_w[:, :], ALU.mult))
                            step(v.tensor_reduce(col_agg[:, t:t + 1], q_val[:, 0, :], AX.X, ALU.add))
                        step(v.tensor_copy(agg_by_col[:, c, :], col_agg[:, :]))
                        ss.restart()
                    dve.wait_ge(slow_to_v, C * (T + 1) + 1)
                    dve.sem_clear(slow_to_v)
                    step(v.tensor_tensor(h2[:, :], h2[:, :], agg[:, :], ALU.add))
                    step(v.memset(w_rank[:, :, :], 0.0))
                    step(v.memset(w_rank_w[:, :], 0.0))
                    ss.restart()

            wire_h = h2[:, :]

            def step(ins):
                st.done(ins)
                st.wait()

            def rows(a, t):
                return a[:, t * N:(t + 1) * N]

            class Sorter:

                def __init__(self, network, wires, spare):
                    self.wire, self.spare, n = list(wires), list(spare), len(wires)
                    self.needed = [n - 1 - r for r in range(int(0.75 * (n - 1)) + 2)]
                    self.layers = pruned(network, self.needed)

                def sort(self, n):
                    wire, spare = self.wire, self.spare
                    for layer in self.layers[:n]:
                        st.wait()
                        for i, (a, b, low, high) in enumerate(layer):
                            if i:
                                st.wait(2)
                            ins = (wire[a], wire[b])
                            if low:
                                wire[a] = spare.pop(0)
                                st.done(v.tensor_tensor(wire[a], ins[0], ins[1], ALU.min))
                            if high:
                                wire[b] = spare.pop(0)
                                st.done(v.tensor_tensor(wire[b], ins[0], ins[1], ALU.max))
                            spare += [w for w in ins if w is not wire_h]
                    st.wait()
                    self.layers = self.layers[n:]

                def top(self):
                    return [self.wire[i] for i in self.needed]

            def stretch(a, b, par):
                marks = [0, 0]

                def x_at(name):
                    assert X_MARKS[marks[0]] == name, name
                    marks[0] += 1
                    dve.sem_inc(x_mark, 1)

                def y_at(name):
                    assert Y_MARKS[marks[1]] == name, name
                    marks[1] += 1
                    dve.sem_inc(y_mark, 1)

                def layer_norm(half, n, src, to, squares):
                    step(v.tensor_reduce(s_sum, tiles(src), AX.X, ALU.add))
                    step(v.scalar_tensor_tensor(tiles(xc), over_c(s_sum), -1.0 / C, tiles(src), ALU.mult, ALU.add))
                    step(v.tensor_tensor(squares[:, :], xc[:, :], xc[:, :], ALU.mult))
                    step(v.tensor_reduce(s_var, tiles(squares), AX.X, ALU.add))
                    dve.sem_inc(var[half], 1)
                    dve.wait_ge(std[half], n)
                    step(v.reciprocal(s_rstd, s_std))
                    step(v.scalar_tensor_tensor(tiles(to), tiles(xc), 0.0, over_c(s_rstd), ALU.max, ALU.mult))

                def split(half, n, src, to):
                    dve.sem_inc(src_ready[half], 1)
                    dve.wait_ge(hi_ready[half], n)
                    step(v.tensor_tensor(tiles(res), tiles(src), to[:, :, 0:C], ALU.subtract))
                    dve.sem_inc(rest_ready[half], 1)
                    dve.wait_ge(mid_ready[half], n)
                    step(v.tensor_tensor(to[:, :, 2 * C:3 * C], tiles(res), to[:, :, C:2 * C], ALU.subtract))

                xb, xa = x[par], x[1 - par]

                def hot(k):
                    if k > 1:
                        dve.wait_ge(gat_full, a * GAT + max(k - 1, 1))
                    step(v.tensor_scalar(one_hot[k % 2][:, :], pos_t[:, :], float(k), None, ALU.is_equal))
                    y_at(f"hot{k}")

                def layer0():
                    dve.wait_ge(root_ready, b + 1)
                    step(v.reciprocal(d0, root))
                    step(v.tensor_scalar(root, root, 1e-7, None, ALU.add))
                    step(v.reciprocal(d1, root))
                    dve.wait_ge(misc_x, b * MISC_X + 1)
                    step(v.tensor_tensor(tiles(y), ps_misc[:, :].rearrange("p (t c) -> p t c", t=T), over_c(d0),
                                         ALU.mult))
                    split(0, b * 5 + 1, y, parts)
                    x_at("parts0")

                def layer0_end():
                    dve.wait_ge(prod_x, b * 4 + 1)
                    step(v.tensor_tensor(y[:, :], y[:, :], ps_prod[:, :], ALU.add))
                    step(v.scalar_tensor_tensor(tiles(y), tiles(y), 0.0, over_c(d0), ALU.max, ALU.mult))
                    step(v.tensor_tensor(xb[:, :], xb[:, :], y[:, :], ALU.add))
                    layer_norm(0, b * 3 + 2, xb, h, y)
                    x_at("h1")

                def propagate(i):
                    src = g_l1[:, :, DEPTH * C:(DEPTH + 1) * C] if i == 1 else tiles(y)
                    step(v.tensor_tensor(tiles(y), src, over_c(d1), ALU.mult))
                    split(0, b * 5 + 1 + i, y, parts)
                    x_at(f"parts{i}")

                def propagated(i):
                    dve.wait_ge(prod_x, b * 4 + 1 + i)
                    step(v.tensor_tensor(y[:, :], y[:, :], ps_prod[:, :], ALU.add))
                    step(v.tensor_tensor(tiles(y), tiles(y), over_c(d1), ALU.mult))
                    step(v.tensor_tensor(tiles(y), tiles(y), g_l1[:, :, (DEPTH - i) * C:(DEPTH - i + 1) * C],
                                         ALU.add))

                def rank(t):
                    dve.wait_ge(cum_full, b * CUM + t + 1)
                    v.tensor_copy(m_all[:, t:t + 1], ps_cum[:, N - 1:N]).then_inc(cum_read_v, 1)
                    v.tensor_tensor(rows(cum, t), ps_cum[:, :], rows(adj_n, t), ALU.mult).then_inc(cum_read_v, 1)

                if a is not None:
                    step(v.tensor_scalar(valid_t[:, :], pos_t[:, :], 1.0, None, ALU.is_ge))
                    y_at("valid")
                    hot(1)
                    hot(2)
                if b is not None:
                    dve.wait_ge(x_loaded, (b + 1) * 16)
                    layer_norm(0, b * 3 + 1, xb, h, y)
                    x_at("h0")
                if a is not None:
                    hot(3)
                if b is not None:
                    layer0()
                    if a is not None:
                        dve.wait_ge(tables_ready, a + 1)
                for i in range(4):
                    if a is not None:
                        hot(4 + i)
                    if b is not None:
                        for t in range(i * T // 4, (i + 1) * T // 4):
                            rank(t)
                if b is not None:
                    dve.wait_ge(misc_x, b * MISC_X + 2)
                    step(v.tensor_tensor(place[:, :], ps_misc[:, 0:T], wide[:, :], ALU.mult))
                    for t in range(T):
                        step(v.tensor_scalar(select[par][:, t, :], places[:, :], place[:, t:t + 1], None,
                                             ALU.is_equal))
                    x_at("select")
                    dve.wait_ge(thresholds_ready, b + 1)
                    dve.wait_ge(cum_read_v, 2 * (b + 1) * T)
                    for t in range(T):
                        step(v.tensor_scalar(rows(keep, t), rows(cum, t), m_drop1[:, t:t + 1], None,
                                             ALU.not_equal))
                        step(v.scalar_tensor_tensor(rows(keep, t), rows(cum, t), m_drop2[:, t:t + 1],
                                                    rows(keep, t), ALU.not_equal, ALU.mult))
                        x_at(f"keep{t}")
                if a is not None:
                    dve.wait_ge(gat_full, a * GAT + SLOTS - 1)
                    for k in range(1, SLOTS):
                        step(v.tensor_scalar(hot_w(k), pos_w[:, :], float(k), None, ALU.is_equal))
                    y_at("hot_w_low")
                    dve.wait_ge(gat_full, a * GAT + SLOTS)
                    for k in range(SLOTS, WIDE):
                        step(v.tensor_scalar(hot_w(k), pos_w[:, :], float(k), None, ALU.is_equal))
                    y_at("hot_w_high")
                if b is not None:
                    layer0_end()
                if a is not None:
                    dve.wait_ge(gat_free, (a + 1) * GAT)
                    dve.wait_ge(weights_ready, a + 1)
                    dve.wait_ge(weights_w_ready, a + 1)
                    slow_v(a)
                    y_at("slow_done")
                    narrow_sort = Sorter(NETWORK_8, [wire_h] + slot[0:SLOTS - 1], slot[SLOTS - 1:])
                    narrow_sort.sort(2)
                if b is not None:
                    dve.wait_ge(misc_x_act, (b + 1) * (T // 2))
                    propagate(1)
                    dve.wait_ge(tr_free, b * TR + 2 * T + 2)
                    for t in range(T):
                        step(v.tensor_tensor(rows(cum, t), rows(cum, t), rows(keep, t), ALU.mult))
                        step(v.tensor_tensor(rows(cum, t), rows(cum, t), rows(keep_t, t), ALU.mult))
                        x_at(f"pos{t}")
                    propagated(1)
                    propagate(2)
                if a is not None:
                    narrow_sort.sort(4)
                if b is not None:
                    propagated(2)
                    propagate(3)
                if a is not None:
                    for r, s in enumerate(narrow_sort.top()):
                        w = over_c(w_rank[:, :, r])
                        if r == 0:
                            step(v.tensor_tensor(tiles(agg), tiles(s), w, ALU.mult))
                        else:
                            step(v.tensor_tensor(tiles(s), tiles(s), w, ALU.mult))
                            step(v.tensor_tensor(agg[:, :], agg[:, :], s, ALU.add))

                    here, there = [slots_w[:, i * WIDE * C:(i + 1) * WIDE * C] for i in range(2)]
                    for layer in range(4):
                        d = 1 << layer
                        lower, upper = [here.rearrange("p (g x y) -> p g x y", x=2, y=d * C)[:, :, i]
                                        for i in range(2)]
                        lo, hi = [there.rearrange("p (g x y) -> p g x y", x=2, y=d * C)[:, :, i] for i in range(2)]
                        st.done(v.tensor_tensor(lo, lower, upper, ALU.min))
                        step(v.tensor_tensor(hi, lower, upper, ALU.max))
                        here, there = there, here
                    wide_sort = Sorter(NETWORK_16[4:], [here[:, i * C:(i + 1) * C] for i in range(WIDE)],
                                       [there[:, i * C:(i + 1) * C] for i in range(WIDE)])
                    wide_sort.sort(6)
                    for r, s in enumerate(wide_sort.top()):
                        if r == 0:
                            step(v.tensor_scalar(agg_w[:, :], s, w_rank_w[:, 0:1], None, ALU.mult))
                        else:
                            step(v.scalar_tensor_tensor(agg_w[:, :], s, w_rank_w[:, r:r + 1], agg_w[:, :],
                                                        ALU.mult, ALU.add))
                    step(v.tensor_copy(parts_w[:, 0:C], agg_w[:, :]))
                    step(v.tensor_tensor(rest_w[:, :], agg_w[:, :], parts_w[:, 0:C], ALU.subtract))
                    step(v.tensor_copy(parts_w[:, C:2 * C], rest_w[:, :]))
                    step(v.tensor_tensor(parts_w[:, 2 * C:3 * C], rest_w[:, :], parts_w[:, C:2 * C],
                                         ALU.subtract))
                    y_at("sorted_w")
                if b is not None:
                    propagated(3)
                    step(v.tensor_tensor(xb[:, :], xb[:, :], y[:, :], ALU.add))
                    step(v.tensor_tensor(tiles(xb), tiles(xb), over_t(bias_l1[:, :]), ALU.add))
                if a is not None:
                    dve.wait_ge(misc_y, a * MISC_Y + 2)
                    step(v.tensor_tensor(agg[:, :], agg[:, :], ps_misc[:, :], ALU.add))
                    step(v.tensor_tensor(agg[:, :], agg[:, :], h2[:, :], ALU.add))
                    y_at("mlp_in")
                if b is not None:
                    layer_norm(0, b * 3 + 3, xb, h2, y)
                    split(0, b * 5 + 5, h2, parts_h2)
                    dve.wait_ge(cum_read_act, (b + 1) * 2)
                    x_at("parts_h2")
                if a is not None:
                    dve.wait_ge(misc_y, a * MISC_Y + 5)
                    step(v.tensor_tensor(tiles(z), ps_misc[:, :].rearrange("p (t c) -> p t c", t=T),
                                         over_t(bias_l2[:, :]), ALU.add))
                    y_at("y_read")
                    step(v.tensor_tensor(tiles(z), tiles(z), over_c(mask_y[:, :]), ALU.mult))
                    step(v.tensor_tensor(xa[:, :], xa[:, :], z[:, :], ALU.add))
                    layer_norm(1, a + 1, xa, h, z)
                    y_at("h3")
                    dve.wait_ge(misc_y, (a + 1) * MISC_Y)
                    step(v.tensor_copy(z[:, :], ps_misc[:, :]))
                    split(1, a + 1, z, parts)
                    y_at("parts_l3")
                    step(v.tensor_tensor(tiles(xa), tiles(xa), over_t(bias_l3[:, :]), ALU.add))
                    dve.wait_ge(prod_y, a + 1)
                    step(v.tensor_tensor(xa[:, :], xa[:, :], ps_prod[:, :], ALU.add))
                    y_at("result")
                st.restart()

            run(dve, stretch)


_INS = ["x", "adj", "nodemask", "L0_gnn_kernel", "L1_gnn_W", "L1_gnn_b", "L2_gnn_W1", "L2_gnn_b1", "L2_gnn_W2",
        "L2_gnn_b2", "L3_gnn_weight", "L3_gnn_bias"]


def kernel(**inputs):
    import numpy as _np
    import concourse.bacc as _bacc
    from concourse import mybir as _mybir
    from concourse.bass_utils import run_bass_kernel_spmd as _run

    nc = _bacc.Bacc("TRN2", target_bir_lowering=False, num_devices=1)
    arrays, args = {}, []
    for name in _INS:
        a = _np.ascontiguousarray(inputs[name])
        if a.dtype == _np.bool_:
            a = a.view(_np.uint8)
        arrays[f"in_{name}"] = a
        args.append(nc.dram_tensor(f"in_{name}", a.shape, _mybir.dt.from_np(a.dtype), kind="ExternalInput").ap())
    shape = inputs["x"].shape
    out = nc.dram_tensor("out", shape, _mybir.dt.float32, kind="ExternalOutput").ap()
    gnn_stack(nc, *args, out)
    r = _run(nc, [arrays], core_ids=[0])
    return r.results[0]["out"]
```

```python
from contextlib import ExitStack

import concourse.bass as bass
from concourse import mybir

NETWORK_8 = [
    [(0, 2), (1, 3), (4, 6), (5, 7)],
    [(0, 4), (1, 5), (2, 6), (3, 7)],
    [(0, 1), (2, 3), (4, 5), (6, 7)],
    [(2, 4), (3, 5)],
    [(1, 4), (3, 6)],
    [(1, 2), (3, 4), (5, 6)],
]
NETWORK_16 = [
    [(i, i + 1) for i in range(0, 16, 2)],
    [(0, 2), (4, 6), (8, 10), (12, 14), (1, 3), (5, 7), (9, 11), (13, 15)],
    [(0, 4), (8, 12), (1, 5), (9, 13), (2, 6), (10, 14), (3, 7), (11, 15)],
    [(i, i + 8) for i in range(8)],
    [(5, 10), (6, 9), (3, 12), (13, 14), (7, 11), (1, 2), (4, 8)],
    [(1, 4), (7, 13), (2, 8), (11, 14)],
    [(2, 4), (5, 6), (9, 10), (11, 13), (3, 8), (7, 12)],
    [(6, 8), (10, 12), (3, 5), (7, 9)],
    [(3, 4), (5, 6), (7, 8), (9, 10), (11, 12)],
    [(6, 7), (8, 9)],
]
SLOTS = 8
WIDE = 16
T_THRESH = 10
ROUND = 8388608.0


def pruned(network, wanted):
    live, out = set(wanted), []
    for layer in reversed(network):
        out.append([(a, b, a in live, b in live) for a, b in layer if a in live or b in live])
        live |= {i for a, b, _, _ in out[-1] for i in (a, b)}
    return out[::-1]


class Steps:

    def __init__(self, engine, sem):
        self.engine, self.sem, self.n = engine, sem, 0

    def restart(self):
        self.wait()
        self.engine.sem_clear(self.sem)
        self.n = 0

    def done(self, ins):
        ins.then_inc(self.sem, 1)
        self.n += 1

    def wait(self, lag=0):
        if self.n > lag:
            self.engine.wait_ge(self.sem, self.n - lag)


def at_least(engine, sem, value):
    if isinstance(value, int) and value <= 0:
        return
    engine.wait_ge(sem, value)


def gnn_stack(nc, x_in, adj, nodemask, w_l0, w_l1, b_l1, w1, b1, w2, b2, w_l3, b_l3, out, limit=WIDE - 1):
    f32, bf16, f16 = mybir.dt.float32, mybir.dt.bfloat16, mybir.dt.float16
    i32, u8 = mybir.dt.int32, mybir.dt.uint8
    ALU, ACT, AX = mybir.AluOpType, mybir.ActivationFunctionType, mybir.AxisListType

    B, N, C = x_in.shape
    P = 128
    T = N // P
    H = w1.shape[1]
    HALF = N // 2
    F = T * C
    DEPTH = 3
    EARLY = 3
    EPS = 1e-5
    RING = 2
    DIAG = N + P

    x_v = x_in.rearrange("b (t p) c -> b p t c", p=P)
    out_v = out.rearrange("b (t p) c -> b p t c", p=P)
    adj_v = adj.rearrange("b (t p) m -> b t p m", p=P)

    ctx = ExitStack()
    with ctx:
        def sb(name, shape, dt):
            return ctx.enter_context(nc.sbuf_tensor(name, shape, dt))

        def pb(name, shape, dt):
            return ctx.enter_context(nc.psum_tensor(name, shape, dt))

        def sem(name):
            return ctx.enter_context(nc.semaphore(name))

        ident_f = sb("ident_f", [P, P], f32)
        ident_b = sb("ident_b", [P, P], bf16)
        ident_h = sb("ident_h", [P, P], f16)
        off_diag = sb("off_diag", [P, P], bf16)
        prefix = sb("prefix", [P, N], bf16)
        ones = prefix[:, P:2 * P]
        ranks = sb("ranks", [P, WIDE], f32)
        places = sb("places", [P, P], f16)
        quant_w = sb("quant_w", [P, 3], f32)
        eps_col = sb("eps_col", [P, 1], f32)
        w_l0_sb = sb("w_l0_sb", [C, C], f32)
        w_l1_sb = sb("w_l1_sb", [C, (DEPTH + 1) * C], f32)
        w1_sb = sb("w1_sb", [C, H], f32)
        b1_sb = sb("b1_sb", [H, 1], f32)
        w2_sb = sb("w2_sb", [H, C], f32)
        w_l3_sb = sb("w_l3_sb", [C, C], f32)
        bias_l1 = sb("bias_l1", [P, C], f32)
        bias_l2 = sb("bias_l2", [P, C], f32)
        bias_l3 = sb("bias_l3", [P, C], f32)
        mask_raw = sb("mask_raw", [B * T, P], u8)
        mask = sb("mask", [P, B, T], f32)
        mask_x = sb("mask_x", [P, T], f32)

        adj_f = sb("adj_f", [P, RING, N], f32)
        adj_n = sb("adj_n", [P, T * N], f16)
        cum = adj_n
        adj_t = [sb(f"adj_t{i}", [P, T * N], bf16) for i in range(2)]
        nbr_diag = sb("nbr_diag", [P, T, P], bf16)
        keep = sb("keep", [P, T * N], f16)
        pos_t = sb("pos_t", [P, T * N], f16)
        one_hot = [sb(f"one_hot{i}", [P, T * N], bf16) for i in range(2)]
        valid_t = one_hot[0]
        keep_t = one_hot[0]
        wide = sb("wide", [P, T], bf16)
        place = sb("place", [P, T], f32)
        select = [sb(f"select{i}", [P, T, P], bf16) for i in range(2)]
        select_t = [sb(f"select_t{i}", [P, N], bf16) for i in range(2)]
        pos_w = sb("pos_w", [P, T * P], f16)
        slots_w = sb("slots_w", [P, 2 * WIDE * C], f32)
        parts_w = sb("parts_w", [P, 3 * C], bf16)
        cnt_b = sb("cnt_b", [P, T], bf16)
        cnt_w = sb("cnt_w", [P, 1], f32)
        w_rank_w = sb("w_rank_w", [P, WIDE], f32)

        x = [sb(f"x{i}", [P, F], f32) for i in range(2)]
        h = sb("h", [P, F], f32)
        h2 = [sb(f"h2_{i}", [P, F], f32) for i in range(2)]
        y = sb("y", [P, F], f32)
        z = sb("z", [P, F], f32)
        res = sb("res", [P, F], f32)
        mask_rows = res[0:B * T, 0:P]
        xc = res
        parts_h2 = sb("parts_h2", [P, T, 3 * C], bf16)
        parts = sb("parts", [P, T, 3 * C], bf16)
        h_t = sb("h_t", [C, N], f32)
        g_l1 = sb("g_l1", [P, T, (DEPTH + 1) * C], f32)
        w_l1_rows = y[0:C, 0:(DEPTH + 1) * C]
        slots = sb("slots", [P, (SLOTS + 4) * F], f32)
        slot = [slots[:, i * F:(i + 1) * F] for i in range(SLOTS + 4)]
        hid_t = slots_w[0:H, 0:N]
        agg = z
        agg_w = h[:, 0:C]
        rest_w = res[:, 0:C]
        stat = sb("stat", [P, 8, T], f32)
        deg, d0, d1, s_sum, s_var, s_std, s_rstd, root = [stat[:, i, :] for i in range(8)]
        dil = sb("dil", [P, 6, T], f32)
        m_all, m_skip, m_do, m_drop1, m_drop2, m_cnt = [dil[:, i, :] for i in range(6)]
        m_max = sb("m_max", [P, 2 * T], f32)[:, :]
        q_pos_w = sb("q_pos_w", [P, 3], f32)
        narrow = sb("narrow", [P, T], f32)
        over = sb("over", [P, 2, T], f32)
        flag = sb("flag", [P, 1], i32)
        q_pos = sb("q_pos", [P, 3, T], f32)
        hat = keep[:, 0:12 * T * SLOTS].bitcast(f32).rearrange("p (a r) -> p a r", a=2)
        hat_w = sb("hat_w", [P, 2, 3 * WIDE], f32)
        w_rank = sb("w_rank", [P, T, SLOTS], f32)

        q_hi = sb("q_hi", [P, 3, T], f32)
        q_frac = sb("q_frac", [P, 3, T], f32)
        col = sb("col", [P, T], f32)
        col_agg = sb("col_agg", [P, T], f32)
        q_val = sb("q_val", [P, 2, 3], f32)

        ps_tr = [pb(f"ps_tr{i}", [P, HALF], f32) for i in range(2)]
        ps_cum = pb("ps_cum", [P, N], f32)
        ps_prod = pb("ps_prod", [P, F], f32)
        ps_gat = pb("ps_gat", [P, 2, HALF], f32)
        ps_misc = pb("ps_misc", [P, HALF], f32)

        const_in = sem("const_in")
        const_pool = sem("const_pool")
        const_pe = sem("const_pe")
        x_loaded = sem("x_loaded")
        adj_loaded = [sem(f"adj_loaded{i}") for i in range(RING)]
        cast_done = sem("cast_done")
        tr_full, tr_free = sem("tr_full"), sem("tr_free")
        cum_full, cum_read_v, cum_read_act = sem("cum_full"), sem("cum_read_v"), sem("cum_read_act")
        prod_x, prod_z = sem("prod_x"), sem("prod_z")
        gat_full, gat_free = sem("gat_full"), sem("gat_free")
        const_act = sem("const_act")
        misc_x, misc_x_act = sem("misc_x"), sem("misc_x_act")
        misc_y, misc_y_act = sem("misc_y"), sem("misc_y_act")
        misc_z, misc_z_act = sem("misc_z"), sem("misc_z_act")
        nbr_ready = sem("nbr_ready")
        wide_ready = sem("wide_ready")
        cnt_ready = sem("cnt_ready")
        thresholds_ready = sem("thresholds_ready")
        tables_ready, weights_ready, weights_w_ready = [sem(n) for n in ("tables_ready", "weights_ready",
                                                                         "weights_w_ready")]
        var, std, src_ready, hi_ready, rest_ready, mid_ready = [
            [sem(f"{n}_{half}") for half in "xz"] for n in ("var", "std", "src", "hi", "rest", "mid")]
        root_ready = sem("root_ready")
        slow_to_pe, slow_to_v = sem("slow_to_pe"), sem("slow_to_v")
        v_step, pool_step = sem("v_step"), sem("pool_step")
        x_mark, y_mark, z_mark = sem("x_mark"), sem("y_mark"), sem("z_mark")
        slow_step = sem("slow_step")
        out_done = sem("out_done")
        settled = sem("settled")

        def tiles(a):
            return a[:, :].rearrange("p (t c) -> p t c", t=T)

        def over_c(s):
            return s.unsqueeze(2).to_broadcast([P, T, C])

        def over_t(row):
            return row.unsqueeze(1).to_broadcast([P, T, C])

        TR_Z = 4
        TR = TR_Z + 3 * T + 4
        CUM = T + 2
        GAT = SLOTS + 2
        MISC_X = 2 + T // 2
        MISC_Y = 2
        MISC_Z = 4

        X_MARKS = (["h0", "parts0", "select", "h1"] + [f"keep{t}" for t in range(T // 2)] + ["parts1"]
                   + [f"keep{t}" for t in range(T // 2, T)]
                   + ["parts2"] + [f"pos{t}" for t in range(T)] + ["parts3", "valid", "hot1", "parts_h2"]
                   + [f"hot{k}" for k in range(2, EARLY + 1)])
        Y_MARKS = ([f"hot{k}" for k in range(EARLY + 1, SLOTS)]
                   + ["hot_w_low", "hot_w_high", "slow_done", "narrow_done", "sorted_w", "mlp_in"])
        Z_MARKS = ["y_read", "h3", "parts_l3", "result"]

        def x_reached(engine, g, name):
            engine.wait_ge(x_mark, g * len(X_MARKS) + X_MARKS.index(name) + 1)

        def y_reached(engine, g, name):
            engine.wait_ge(y_mark, g * len(Y_MARKS) + Y_MARKS.index(name) + 1)

        def z_reached(engine, g, name):
            engine.wait_ge(z_mark, g * len(Z_MARKS) + Z_MARKS.index(name) + 1)

        def run(engine, stretch):
            stretch(None, None, 0, 0, 0)
            stretch(None, 0, 1, 1, TR)
            if B > 2:
                with engine.Fori(0, (B - 2) // 2) as i:
                    stretch(i * 2, i * 2 + 1, i * 2 + 2, 0, (i * 2 + 2) * TR)
                    stretch(i * 2 + 1, i * 2 + 2, i * 2 + 3, 1, (i * 2 + 3) * TR)
            stretch(B - 2, B - 1, None, 0, B * TR)
            stretch(B - 1, None, None, 1, B * TR + TR_Z)

        def hot_w(k):
            return one_hot[k // SLOTS][:, k % SLOTS * N:(k % SLOTS + 1) * N]

        def settle(engine):
            engine.sem_inc(settled, 1)

        block = ctx.enter_context(nc.Block())

        @block.sync
        def _(sp):
            for dst, src in [(w_l0_sb[:, :], w_l0), (w_l1_rows[:, :], w_l1), (w1_sb[:, :], w1),
                             (b1_sb[:, :], b1.unsqueeze(1)), (w2_sb[:, :], w2), (w_l3_sb[:, :], w_l3),
                             (bias_l1[:, :], b_l1.partition_broadcast(P)), (bias_l2[:, :], b2.partition_broadcast(P)),
                             (bias_l3[:, :], b_l3.partition_broadcast(P)),
                             (mask_raw[:, :], nodemask.rearrange("b (t p) -> (b t) p", p=P))]:
                sp.dma_start(dst, src).then_inc(const_in, 16)

            def load_rows(g, tile_range):
                for t in tile_range:
                    at_least(sp, cast_done, g * T + (t + 1 - RING))
                    settle(sp)
                    sp.dma_start(adj_f[:, t % RING, :], adj_v[g, t]).then_inc(adj_loaded[t % RING], 16)

            def stretch(c, a, b, par, tr):
                if b is not None:
                    load_rows(b, range(T // 2))
                if c is not None:
                    z_reached(sp, c, "result")
                    settle(sp)
                    sp.dma_start(out_v[c], tiles(x[par])).then_inc(out_done, 16)
                    sp.wait_ge(out_done, (c + 1) * 16)
                    settle(sp)
                if b is not None:
                    sp.dma_start(tiles(x[par]), x_v[b]).then_inc(x_loaded, 16)
                    load_rows(b, range(T // 2, T))

            run(sp, stretch)

        @block.gpsimd
        def _(pool):
            st = Steps(pool, pool_step)

            def step(ins):
                st.done(ins)
                st.wait()

            for m in (ident_f, ident_b, ident_h):
                step(pool.memset(m[:, :], 0.0))
                step(pool.affine_select(out=m[:, :], in_=m[:, :], compare_op=ALU.not_equal, fill=1.0, base=0,
                                        pattern=[[-1, P]], channel_multiplier=1))
            step(pool.memset(off_diag[:, :], 1.0))
            step(pool.affine_select(out=off_diag[:, :], in_=off_diag[:, :], compare_op=ALU.not_equal, fill=0.0,
                                    base=0, pattern=[[-1, P]], channel_multiplier=1))
            step(pool.memset(prefix[:, :], 1.0))
            step(pool.affine_select(out=prefix[:, 0:P], in_=prefix[:, 0:P], compare_op=ALU.is_ge, fill=0.0, base=0,
                                    pattern=[[1, P]], channel_multiplier=-1))
            step(pool.memset(eps_col[:, :], EPS))
            step(pool.iota(places[:, :], [[1, P]], base=1, channel_multiplier=0,
                           allow_small_or_imprecise_dtypes=True))
            for r in range(WIDE):
                step(pool.memset(ranks[:, r:r + 1], float(r)))
            for q, w in enumerate((0.25, 0.5, 0.25)):
                step(pool.memset(quant_w[:, q:q + 1], w))
            pool.wait_ge(const_in, 160)
            step(pool.tensor_copy(mask_rows[:, :], mask_raw[:, :]))
            pool.sem_inc(const_pool, 1)

            def diagonals(dst, src, factor, op):
                rows = src[:, 0:(T - 1) * DIAG].rearrange("p (t s) -> p t s", s=DIAG)[:, :, 0:P]
                to = dst[0] if isinstance(dst, tuple) else dst[:, 0:(T - 1) * DIAG].rearrange(
                    "p (t s) -> p t s", s=DIAG)[:, :, 0:P]
                last = dst[1] if isinstance(dst, tuple) else dst[:, (T - 1) * DIAG:T * N]
                st.done(pool.tensor_tensor(to, rows, factor[:, :].unsqueeze(1).to_broadcast([P, T - 1, P]), op))
                st.done(pool.tensor_tensor(last, src[:, (T - 1) * DIAG:T * N], factor[:, :], op))

            def rank_weights(out, hat, groups, n_ranks, positions):
                size = 3 * groups * n_ranks
                a, c = [hat[:, i, 0:size].rearrange("p (t r) -> p t r", r=n_ranks) for i in range(2)]
                step(pool.tensor_tensor(a, ranks[:, 0:n_ranks].unsqueeze(1).to_broadcast([P, 3 * groups, n_ranks]),
                                        positions.unsqueeze(2).to_broadcast([P, 3 * groups, n_ranks]), ALU.subtract))
                step(pool.tensor_scalar(c, a, 0.0, None, ALU.max))
                step(pool.tensor_scalar(a, a, 0.0, None, ALU.min))
                step(pool.tensor_tensor(a, a, c, ALU.subtract))
                step(pool.tensor_scalar(a, a, 1.0, None, ALU.add))
                step(pool.tensor_scalar(a, a, 0.0, 0.25, ALU.max, ALU.mult))
                q = hat[:, 0, 0:size].rearrange("p (q t r) -> p q t r", q=3, r=n_ranks)
                step(pool.tensor_tensor(out, q[:, 0], q[:, 2], ALU.add))
                step(pool.tensor_tensor(out, out, q[:, 1], ALU.add))
                step(pool.tensor_tensor(out, out, q[:, 1], ALU.add))

            def part_x(g, par):
                pool.wait_ge(tr_full, g * TR + TR_Z + T)
                diagonals(adj_n, adj_n, off_diag, ALU.mult)
                pool.wait_ge(tr_free, g * TR + TR_Z + T)
                diagonals((nbr_diag[:, 0:T - 1, :], nbr_diag[:, T - 1, :]), adj_t[par], off_diag, ALU.mult)
                st.wait()
                pool.sem_inc(nbr_ready, 1)

                pool.wait_ge(cum_read_v, 2 * (g + 1) * T)
                settle(pool)
                step(pool.tensor_scalar(wide[:, :], m_all, float(SLOTS - 1), None, ALU.is_gt))
                pool.sem_inc(wide_ready, 1)
                step(pool.tensor_copy(mask_x[:, :], mask[:, g, :]))
                step(pool.tensor_scalar(m_skip, m_all, 0.5, 0.25, ALU.mult, ALU.add))
                step(pool.tensor_scalar(m_skip, m_skip, ROUND, ROUND, ALU.add, ALU.subtract))
                step(pool.tensor_scalar(m_do, m_all, float(T_THRESH), None, ALU.is_gt))
                step(pool.tensor_tensor(m_do, m_do, mask_x[:, :], ALU.mult))
                step(pool.tensor_tensor(m_skip, m_skip, m_do, ALU.mult))
                step(pool.tensor_tensor(m_skip, m_skip, m_do, ALU.add))
                step(pool.tensor_scalar(m_drop1, m_skip, -1.0, None, ALU.add))
                step(pool.tensor_scalar(m_drop2, m_drop1, 2.0, None, ALU.mult))
                pool.sem_inc(thresholds_ready, 1)
            def part_y_narrow(g, before):
                pool.wait_ge(gat_free, g * GAT + 1)
                settle(pool)
                step(pool.tensor_copy(cnt_b[:, :], m_cnt))
                pool.sem_inc(cnt_ready, 1)
                step(pool.tensor_scalar(narrow[:, :], m_all, float(SLOTS - 1), None, ALU.is_le))
                step(pool.tensor_scalar(m_max[:, 0:T], m_all, float(limit), None, ALU.is_gt))
                step(pool.tensor_scalar(m_max[:, T:2 * T], narrow[:, :], -1.0, 1.0, ALU.mult, ALU.add))
                step(pool.partition_all_reduce(over[:, :, :].rearrange("p a t -> p (a t)"), m_max, P,
                                               bass.bass_isa.ReduceOp.add))
                half = T // 2
                while half:
                    step(pool.tensor_tensor(over[:, :, 0:half], over[:, :, 0:half], over[:, :, half:2 * half],
                                            ALU.add))
                    half //= 2
                step(pool.tensor_scalar(over[:, 1, 0:1], over[:, 1, 0:1], float(P), None, ALU.is_gt))
                step(pool.tensor_tensor(over[:, 0, 0:1], over[:, 0, 0:1], over[:, 1, 0:1], ALU.add))
                step(pool.tensor_scalar(over[:, 0, 0:1], over[:, 0, 0:1], 0.0, None, ALU.is_gt))
                step(pool.tensor_copy(flag[:, :], over[:, 0, 0:1]))

                pool.sem_inc(tables_ready, 1)
                if before is not None:
                    y_reached(pool, before, "narrow_done")
                    settle(pool)
                for q, tau in enumerate((0.25, 0.5, 0.75)):
                    step(pool.tensor_scalar(q_pos[:, q, :], m_cnt, tau, None, ALU.mult))
                rank_weights(w_rank[:, :, :], hat, T, SLOTS, q_pos[:, :, :].rearrange("p q t -> p (q t)"))
                step(pool.tensor_tensor(w_rank[:, :, :], w_rank[:, :, :],
                                        narrow[:, :].unsqueeze(2).to_broadcast([P, T, SLOTS]), ALU.mult))
                pool.sem_inc(weights_ready, 1)

            def part_y_wide(g):
                pool.wait_ge(misc_y_act, g + 1)
                settle(pool)
                for q, tau in enumerate((0.25, 0.5, 0.75)):
                    step(pool.tensor_scalar(q_pos_w[:, q:q + 1], cnt_w[:, :], tau, None, ALU.mult))
                rank_weights(w_rank_w[:, :].unsqueeze(1), hat_w, 1, WIDE, q_pos_w[:, :])
                pool.sem_inc(weights_w_ready, 1)

            def stretch(c, a, b, par, tr):
                st.restart()
                if a is not None:
                    part_y_narrow(a, c)
                if a is not None:
                    part_y_wide(a)
                if b is not None:
                    part_x(b, par)

            run(pool, stretch)

        @block.scalar
        def _(act):
            act.wait_ge(const_pool, 1)
            act.wait_ge(const_pe, 2)
            act.activation(mask[:, :, :].rearrange("p b t -> p (b t)"), ps_misc[:, 0:B * T], ACT.Copy)\
               .then_inc(const_act, 1)
            act.activation(w_l1_sb[:, :], ps_prod[0:C, 0:(DEPTH + 1) * C], ACT.Copy).then_inc(const_act, 1)

            def stretch(c, a, b, par, tr):
                def from_tr(n, dst, bank_view):
                    act.wait_ge(tr_full, n)
                    act.activation(dst, bank_view, ACT.Copy).then_inc(tr_free, 1)

                def from_tiles(n, dst, t):
                    bank = ps_tr[t % 2][:, :].bitcast(f16).rearrange("p (j n) -> p j n", j=T)
                    from_tr(n + t, dst[:, :].rearrange("p (j n) -> p j n", j=T)[:, :, t * P:(t + 1) * P], bank)

                def feature_rows(n):
                    for i in range(2):
                        from_tr(n + i, h_t[:, i * HALF:(i + 1) * HALF], ps_tr[i][0:C, :])

                def deviation(half, n):
                    act.wait_ge(var[half], n)
                    act.activation(s_std, s_var, ACT.Sqrt, bias=eps_col[:, :], scale=1.0 / C).then_inc(std[half], 1)

                def split(half, n, src, to):
                    act.wait_ge(src_ready[half], n)
                    act.activation(to[:, :, 0:C], tiles(src), ACT.Copy).then_inc(hi_ready[half], 1)
                    act.wait_ge(rest_ready[half], n)
                    act.activation(to[:, :, C:2 * C], tiles(res), ACT.Copy).then_inc(mid_ready[half], 1)

                def cast(t):
                    act.wait_ge(adj_loaded[t % RING], b * (T // RING * 16) + (t // RING + 1) * 16)
                    act.activation(adj_n[:, t * N:(t + 1) * N], adj_f[:, t % RING, :], ACT.Copy,
                                   accum_out=deg[:, t:t + 1]).then_inc(cast_done, 1)

                def narrow_slot(g, k):
                    act.wait_ge(gat_full, g * GAT + k + 1)
                    act.activation(slot[k - 1][:, :], ps_gat[:, k % 2, :], ACT.Copy).then_inc(gat_free, 1)

                tr_x = tr + TR_Z
                if c is None:
                    at_least(act, tr_free, tr)
                    act.sem_inc(tr_free, TR_Z)
                if c is not None:
                    feature_rows(tr + 1)
                    for i in range(2):
                        act.wait_ge(misc_z, c * MISC_Z + 1 + i)
                        act.activation(hid_t[:, i * HALF:(i + 1) * HALF], ps_misc[:, :], ACT.Relu,
                                       bias=b1_sb[:, :]).then_inc(misc_z_act, 1)
                if b is not None:
                    cast(0)
                    cast(1)
                if c is not None:
                    deviation(1, c + 1)
                if a is not None:
                    narrow_slot(a, 4)
                if c is not None:
                    feature_rows(tr + 3)
                    split(1, c + 1, z, parts)
                if a is not None:
                    narrow_slot(a, 5)
                if b is not None:
                    cast(2)
                    cast(3)
                if a is not None:
                    narrow_slot(a, 6)
                    narrow_slot(a, 7)
                    for i in range(2):
                        act.wait_ge(gat_full, a * GAT + SLOTS + i + 1)
                        act.activation(slots_w[:, i * HALF:(i + 1) * HALF], ps_gat[:, i, :], ACT.Copy)\
                           .then_inc(gat_free, 1)
                    act.wait_ge(misc_y, a * MISC_Y + 1)
                    act.activation(cnt_w[:, :], ps_misc[:, 0:1], ACT.Copy).then_inc(misc_y_act, 1)
                if b is not None:
                    for t in range(T):
                        if t == 2:
                            deviation(0, b * 3 + 1)
                        from_tiles(tr_x + 1, adj_t[par], t)
                        if t + 4 < T:
                            cast(t + 4)
                    act.wait_ge(cast_done, (b + 1) * T)
                    act.activation(root, deg, ACT.Sqrt, bias=1.0).then_inc(root_ready, 1)
                    feature_rows(tr_x + T + 1)
                    split(0, b * 5 + 1, y, parts)
                    deviation(0, b * 3 + 2)
                    feature_rows(tr_x + T + 3)
                    for i in range(T // 2):
                        act.wait_ge(misc_x, b * MISC_X + 3 + i)
                        act.activation(g_l1[:, 2 * i:2 * i + 2, :],
                                       ps_misc[:, :].rearrange("p (t c) -> p t c", t=2), ACT.Copy)\
                           .then_inc(misc_x_act, 1)
                    split(0, b * 5 + 2, y, parts)
                    if a is not None:
                        y_reached(act, a, "slow_done")
                    for t in range(T):
                        from_tiles(tr_x + T + 5, keep_t, t)
                    act.wait_ge(cum_full, b * CUM + T + 1)
                    act.activation(select_t[par][:, :], ps_cum[:, 0:HALF].bitcast(bf16), ACT.Copy)\
                       .then_inc(cum_read_act, 1)
                    split(0, b * 5 + 3, y, parts)
                    for t in range(T):
                        from_tiles(tr_x + 2 * T + 5, pos_t, t)
                    split(0, b * 5 + 4, y, parts)
                    act.wait_ge(cum_full, (b + 1) * CUM)
                    act.activation(pos_w[:, :], ps_cum[:, :], ACT.Copy).then_inc(cum_read_act, 1)
                    deviation(0, b * 3 + 3)
                    split(0, b * 5 + 5, h2[par], parts_h2)
                    act.wait_ge(gat_full, b * GAT + 1)
                    act.activation(m_cnt, ps_gat[:, 0, 0:T], ACT.Copy).then_inc(gat_free, 1)
                    if a is not None:
                        y_reached(act, a, "narrow_done")
                    for k in range(1, EARLY + 1):
                        narrow_slot(b, k)

            run(act, stretch)

        @block.tensor
        def _(pe):
            pe.wait_ge(const_pool, 1)
            nc.tensor.transpose(ps_misc[:, 0:B * T], mask_rows[:, :], ident_f[0:B * T, 0:B * T]).then_inc(const_pe, 1)
            for i in range(DEPTH + 1):
                last = nc.tensor.transpose(ps_prod[0:C, i * C:(i + 1) * C], w_l1_rows[:, i * C:(i + 1) * C],
                                           ident_f[0:C, 0:C])
            last.then_inc(const_pe, 1)
            pe.wait_ge(const_act, 2)

            def stretch(c, a, b, par, tr):
                tr_x = tr + TR_Z

                def transpose_tile(n, src, t):
                    at_least(pe, tr_free, n + t - 1)
                    view = ps_tr[t % 2][:, :].bitcast(f16).rearrange("p (j n) -> p j n", j=T)
                    for j in range(T):
                        last = nc.tensor.transpose(view[:, j, :], src[:, t * N + j * P:t * N + (j + 1) * P],
                                                   ident_h[:, :])
                    last.then_inc(tr_full, 1)

                def transpose_features(n, src):
                    for i in range(2):
                        pe.wait_ge(tr_free, n + i - 1)
                        settle(pe)
                        for t in range(T // 2):
                            tt = i * (T // 2) + t
                            last = nc.tensor.transpose(ps_tr[i][0:C, t * P:(t + 1) * P],
                                                       src[:, tt * C:(tt + 1) * C], ident_f[:, :])
                        last.then_inc(tr_full, 1)
                    pe.wait_ge(tr_free, n + 2)

                def product(dst, lhs_t, rhs, signal):
                    for t in range(T):
                        for j in range(T):
                            for k in range(3):
                                last = nc.tensor.matmul(dst[:, t * C:(t + 1) * C],
                                                        lhs_t[:, j * N + t * P:j * N + (t + 1) * P],
                                                        rhs[:, j, k * C:(k + 1) * C],
                                                        start=(j == 0 and k == 0), stop=(j == T - 1 and k == 2))
                    last.then_inc(signal, 1)

                def node_linear(w_sb, signal):
                    for t in range(T):
                        last = nc.tensor.matmul(ps_misc[:, t * C:(t + 1) * C], h_t[:, t * P:(t + 1) * P],
                                                w_sb[:, :], start=True, stop=True)
                    last.then_inc(signal, 1)

                def ranks_of(t):
                    at_least(pe, cum_read_act, b * 2)
                    for half in range(2):
                        at_least(pe, cum_read_v, 2 * (b * T + t) - 1 + half)
                        lo = half * HALF
                        js = [j for j in range(T) if j * P < lo + HALF]
                        for j in js:
                            start = max(lo, j * P)
                            lhs = (nbr_diag[:, t, :] if j == t
                                   else adj_t[par][:, j * N + t * P:j * N + (t + 1) * P])
                            last = nc.tensor.matmul(ps_cum[:, start:lo + HALF], lhs,
                                                    prefix[:, start - j * P:lo + HALF - j * P],
                                                    start=(j == 0), stop=(j == js[-1]))
                    last.then_inc(cum_full, 1)

                def transpose_adjacency(t):
                    pe.wait_ge(cast_done, b * T + t + 1)
                    transpose_tile(tr_x, adj_n, t)

                def gather(g, k):
                    if k <= EARLY:
                        x_reached(pe, g, f"hot{k}" if k > 1 else "parts_h2")
                    else:
                        y_reached(pe, g, f"hot{k}")
                    if k > 1:
                        pe.wait_ge(gat_free, g * GAT + k - 1)
                    product(ps_gat[:, k % 2, :], one_hot[k % 2], parts_h2, gat_full)

                def wide_slot(bank, at, lhs_of):
                    for j in range(T):
                        for k in range(3):
                            last = nc.tensor.matmul(ps_gat[:, bank, at * C:(at + 1) * C], lhs_of(j),
                                                    parts_h2[:, j, k * C:(k + 1) * C],
                                                    start=(j == 0 and k == 0), stop=(j == T - 1 and k == 2))
                    return last

                if c is None:
                    at_least(pe, tr_free, tr)
                    pe.sem_inc(tr_full, TR_Z)
                if c is not None:
                    y_reached(pe, c, "mlp_in")
                    transpose_features(tr, agg)
                    for i in range(2):
                        if i:
                            pe.wait_ge(misc_z_act, c * 2 + 1)
                        nc.tensor.matmul(ps_misc[:, :], w1_sb[:, :], h_t[:, i * HALF:(i + 1) * HALF],
                                         start=True, stop=True).then_inc(misc_z, 1)
                    pe.wait_ge(misc_z_act, (c + 1) * 2)
                    for t in range(T):
                        last = nc.tensor.matmul(ps_misc[:, t * C:(t + 1) * C], hid_t[:, t * P:(t + 1) * P],
                                                w2_sb[:, :], start=True, stop=True)
                    last.then_inc(misc_z, 1)
                if a is not None:
                    gather(a, 4)
                if c is not None:
                    z_reached(pe, c, "h3")
                    transpose_features(tr + 2, h)
                    node_linear(w_l3_sb, misc_z)
                if a is not None:
                    gather(a, 5)
                if c is not None:
                    z_reached(pe, c, "parts_l3")
                    product(ps_prod, adj_t[par], parts, prod_z)
                if a is not None:
                    gather(a, 6)
                    gather(a, 7)
                    pe.wait_ge(gat_free, a * GAT + SLOTS - 1)
                    wide_slot(0, 0, lambda j: select[1 - par][:, j, :])
                    y_reached(pe, a, "hot_w_low")
                    for k in range(1, SLOTS):
                        last = wide_slot(0, k, lambda j: hot_w(k)[:, j * P:(j + 1) * P])
                    last.then_inc(gat_full, 1)
                    pe.wait_ge(gat_free, a * GAT + SLOTS)
                    y_reached(pe, a, "hot_w_high")
                    for k in range(SLOTS, WIDE):
                        last = wide_slot(1, k - SLOTS, lambda j: hot_w(k)[:, j * P:(j + 1) * P])
                    last.then_inc(gat_full, 1)
                    pe.wait_ge(cnt_ready, a + 1)
                    for t in range(T):
                        last = nc.tensor.matmul(ps_misc[:, 0:1], select[1 - par][:, t, :], cnt_b[:, t:t + 1],
                                                start=(t == 0), stop=(t == T - 1))
                    last.then_inc(misc_y, 1)
                if b is not None:
                    for t in range(T):
                        transpose_adjacency(t)
                if a is not None:
                    slow_pe(pe, a)
                if b is not None:
                    if a is not None:
                        pe.wait_ge(misc_y_act, a + 1)
                    x_reached(pe, b, "h0")
                    transpose_features(tr_x + T, h)
                    node_linear(w_l0_sb, misc_x)
                    pe.wait_ge(nbr_ready, b + 1)
                    for t in range(T):
                        ranks_of(t)
                    x_reached(pe, b, "parts0")
                    pe.wait_ge(wide_ready, b + 1)
                    nc.tensor.matmul(ps_misc[:, 0:T], prefix[:, 0:P], wide[:, :], start=True, stop=False)
                    for t in range(1, T):
                        last = nc.tensor.matmul(ps_misc[:, t:T], ones[:, :], wide[:, 0:T - t],
                                                start=False, stop=(t == T - 1))
                    last.then_inc(misc_x, 1)
                if b is not None:
                    product(ps_prod, adj_t[par], parts, prod_x)
                if b is not None:
                    x_reached(pe, b, "h1")
                    transpose_features(tr_x + T + 2, h)
                    for i in range(T // 2):
                        if i:
                            pe.wait_ge(misc_x_act, b * (T // 2) + i)
                        for t in range(2):
                            tt = 2 * i + t
                            last = nc.tensor.matmul(ps_misc[:, t * 4 * C:(t + 1) * 4 * C],
                                                    h_t[:, tt * P:(tt + 1) * P], w_l1_sb[:, :],
                                                    start=True, stop=True)
                        last.then_inc(misc_x, 1)
                    x_reached(pe, b, "parts1")
                    product(ps_prod, adj_t[par], parts, prod_x)
                    for t in range(T):
                        x_reached(pe, b, f"keep{t}")
                        transpose_tile(tr_x + T + 4, keep, t)
                    pe.wait_ge(cum_read_v, 2 * (b + 1) * T)
                    for t in range(T):
                        last = nc.tensor.transpose(ps_cum[:, t * (P // 2):(t + 1) * (P // 2)].bitcast(bf16),
                                                   select[par][:, t, :], ident_b[:, :])
                    last.then_inc(cum_full, 1)
                    x_reached(pe, b, "parts2")
                    product(ps_prod, adj_t[par], parts, prod_x)
                    for t in range(T):
                        x_reached(pe, b, f"pos{t}")
                        transpose_tile(tr_x + 2 * T + 4, cum, t)
                    pe.wait_ge(cum_read_act, b * 2 + 1)
                    for j in range(T):
                        for t in range(T):
                            last = nc.tensor.matmul(ps_cum[:, j * P:(j + 1) * P],
                                                    cum[:, t * N + j * P:t * N + (j + 1) * P],
                                                    select[par][:, t, :], start=(t == 0), stop=(t == T - 1))
                    last.then_inc(cum_full, 1)
                    x_reached(pe, b, "parts3")
                    product(ps_prod, adj_t[par], parts, prod_x)
                    x_reached(pe, b, "valid")
                    for t in range(T):
                        for j in range(T):
                            last = nc.tensor.matmul(ps_gat[:, 0, t:t + 1],
                                                    valid_t[:, j * N + t * P:j * N + (t + 1) * P],
                                                    ones[:, 0:1], start=(j == 0), stop=(j == T - 1))
                    last.then_inc(gat_full, 1)
                    for k in range(1, EARLY + 1):
                        gather(b, k)
                if a is not None:
                    y_reached(pe, a, "sorted_w")
                    if b is not None:
                        pe.wait_ge(misc_x_act, (b + 1) * (T // 2))
                    for t in range(T):
                        for k in range(3):
                            last = nc.tensor.matmul(ps_misc[:, t * C:(t + 1) * C],
                                                    select_t[1 - par][:, t * P:(t + 1) * P],
                                                    parts_w[:, k * C:(k + 1) * C], start=(k == 0), stop=(k == 2))
                    last.then_inc(misc_y, 1)
            def slow_pe(pe, g):
                pe.wait_ge(tables_ready, g + 1)
                settle(pe)
                many = pe.value_load(flag[0:1, 0:1], min_val=0, max_val=1)
                with pe.If(many > 0):
                    with pe.Fori(0, C) as c:
                        pe.wait_ge(slow_to_pe, c * (T + 2) + 1)
                        for t in range(T):
                            last = nc.tensor.transpose(ps_gat[:, t // (T // 2), (t % (T // 2)) * P:(t % (T // 2) + 1) * P],
                                                       col[:, t:t + 1].to_broadcast([P, P]), ident_f[:, :])
                        last.then_inc(slow_to_v, 1)
                        for t in range(T):
                            pe.wait_ge(slow_to_pe, c * (T + 2) + t + 2)
                            for half in range(2):
                                for j in range(T):
                                    last = nc.tensor.matmul(
                                        ps_gat[:, half, :], valid_t[:, j * N + t * P:j * N + (t + 1) * P],
                                        one_hot[1][:, j * N + half * HALF:j * N + (half + 1) * HALF],
                                        start=(j == 0), stop=(j == T - 1))
                            last.then_inc(slow_to_v, 1)
                        pe.wait_ge(slow_to_pe, c * (T + 2) + T + 2)
                    pe.sem_clear(slow_to_pe)
                    pe.drain().then_inc(slow_to_v, 1)

            run(pe, stretch)

        @block.vector
        def _(dve):
            v = nc.vector
            st = Steps(dve, v_step)
            dve.wait_ge(const_pool, 1)
            dve.wait_ge(const_in, 160)
            dve.wait_ge(const_act, 2)

            def slow_v(g, h_in):
                settle(dve)
                many = dve.value_load(flag[0:1, 0:1], min_val=0, max_val=1)
                with dve.If(many > 0):
                    ss = Steps(dve, slow_step)

                    def step(ins):
                        ss.done(ins)
                        ss.wait()

                    spread, masked = slots[:, 0:N], slots[:, N:2 * N]
                    step(v.tensor_scalar(valid_t[:, :], pos_t[:, :], 1.0, None, ALU.is_ge))
                    for t in range(T):
                        block_t = valid_t[:, t * DIAG:t * DIAG + P]
                        step(v.tensor_tensor(block_t, block_t, ident_b[:, :], ALU.add))
                    step(v.tensor_scalar(q_hi[:, :, :], q_pos[:, :, :], 1.0, None, ALU.add))
                    step(v.tensor_scalar(q_frac[:, :, :], q_pos[:, :, :], 0.375, None, ALU.subtract))
                    step(v.tensor_scalar(q_frac[:, :, :], q_frac[:, :, :], ROUND, ROUND, ALU.add, ALU.subtract))
                    step(v.tensor_tensor(q_frac[:, :, :], q_pos[:, :, :], q_frac[:, :, :], ALU.subtract))
                    ss.restart()
                    h_by_col = h_in[:, :].rearrange("p (t c) -> p c t", t=T)
                    agg_by_col = agg[:, :].rearrange("p (t c) -> p c t", t=T)
                    with dve.Fori(0, C) as c:
                        step(v.tensor_copy(col[:, :], h_by_col[:, c, :]))
                        dve.sem_inc(slow_to_pe, 1)
                        dve.wait_ge(slow_to_v, c * (T + 1) + 1)
                        step(v.tensor_copy(spread.rearrange("p (a n) -> p a n", a=2), ps_gat[:, :, :]))
                        for j in range(T):
                            step(v.tensor_scalar(one_hot[1][:, j * N:(j + 1) * N], spread, col[:, j:j + 1], None,
                                                 ALU.is_gt))
                        dve.sem_inc(slow_to_pe, 1)
                        for t in range(T):
                            dve.wait_ge(slow_to_v, c * (T + 1) + 2 + t)
                            for q in range(3):
                                for hi, (bound, op) in enumerate(((q_pos, ALU.is_le), (q_hi, ALU.is_lt))):
                                    step(v.scalar_tensor_tensor(
                                        masked.rearrange("p (a n) -> p a n", a=2), ps_gat[:, :, :],
                                        bound[:, q, t:t + 1], spread.rearrange("p (a n) -> p a n", a=2), op, ALU.mult))
                                    step(v.tensor_reduce(q_val[:, hi, q:q + 1], masked, AX.X, ALU.max))
                            dve.sem_inc(slow_to_pe, 1)
                            step(v.tensor_tensor(q_val[:, 1, :], q_val[:, 1, :], q_val[:, 0, :], ALU.subtract))
                            step(v.tensor_tensor(q_val[:, 1, :], q_val[:, 1, :], q_frac[:, :, t], ALU.mult))
                            step(v.tensor_tensor(q_val[:, 0, :], q_val[:, 1, :], q_val[:, 0, :], ALU.add))
                            step(v.tensor_tensor(q_val[:, 0, :], q_val[:, 0, :], quant_w[:, :], ALU.mult))
                            step(v.tensor_reduce(col_agg[:, t:t + 1], q_val[:, 0, :], AX.X, ALU.add))
                        step(v.tensor_copy(agg_by_col[:, c, :], col_agg[:, :]))
                        ss.restart()
                    dve.wait_ge(slow_to_v, C * (T + 1) + 1)
                    dve.sem_clear(slow_to_v)
                    step(v.tensor_tensor(h_in[:, :], h_in[:, :], agg[:, :], ALU.add))
                    step(v.memset(w_rank[:, :, :], 0.0))
                    dve.wait_ge(weights_w_ready, g + 1)
                    step(v.memset(w_rank_w[:, :], 0.0))
                    ss.restart()


            def step(ins):
                st.done(ins)
                st.wait()

            def rows(a, t):
                return a[:, t * N:(t + 1) * N]

            class Sorter:

                def __init__(self, network, wires, spare, kept=None):
                    self.wire, self.spare, self.kept, n = list(wires), list(spare), kept, len(wires)
                    self.needed = [n - 1 - r for r in range(int(0.75 * (n - 1)) + 2)]
                    self.layers = pruned(network, self.needed)

                def sort(self, n):
                    wire, spare = self.wire, self.spare
                    for layer in self.layers[:n]:
                        st.wait()
                        for i, (a, b, low, high) in enumerate(layer):
                            if i:
                                st.wait(2)
                            ins = (wire[a], wire[b])
                            if low:
                                wire[a] = spare.pop(0)
                                st.done(v.tensor_tensor(wire[a], ins[0], ins[1], ALU.min))
                            if high:
                                wire[b] = spare.pop(0)
                                st.done(v.tensor_tensor(wire[b], ins[0], ins[1], ALU.max))
                            spare += [w for w in ins if w is not self.kept]
                    st.wait()
                    self.layers = self.layers[n:]

                def top(self):
                    return [self.wire[i] for i in self.needed]

            def stretch(c, a, b, par, tr):
                marks = [0, 0, 0]
                tr_x = tr + TR_Z

                def x_at(name):
                    assert X_MARKS[marks[0]] == name, name
                    marks[0] += 1
                    dve.sem_inc(x_mark, 1)

                def y_at(name):
                    assert Y_MARKS[marks[1]] == name, name
                    marks[1] += 1
                    dve.sem_inc(y_mark, 1)

                def z_at(name):
                    assert Z_MARKS[marks[2]] == name, name
                    marks[2] += 1
                    dve.sem_inc(z_mark, 1)

                def layer_norm(half, n, src, to, squares):
                    step(v.tensor_reduce(s_sum, tiles(src), AX.X, ALU.add))
                    step(v.scalar_tensor_tensor(tiles(xc), over_c(s_sum), -1.0 / C, tiles(src), ALU.mult, ALU.add))
                    step(v.tensor_tensor(squares[:, :], xc[:, :], xc[:, :], ALU.mult))
                    step(v.tensor_reduce(s_var, tiles(squares), AX.X, ALU.add))
                    dve.sem_inc(var[half], 1)
                    dve.wait_ge(std[half], n)
                    step(v.reciprocal(s_rstd, s_std))
                    step(v.scalar_tensor_tensor(tiles(to), tiles(xc), 0.0, over_c(s_rstd), ALU.max, ALU.mult))

                def split(half, n, src, to):
                    dve.sem_inc(src_ready[half], 1)
                    dve.wait_ge(hi_ready[half], n)
                    step(v.tensor_tensor(tiles(res), tiles(src), to[:, :, 0:C], ALU.subtract))
                    dve.sem_inc(rest_ready[half], 1)
                    dve.wait_ge(mid_ready[half], n)
                    step(v.tensor_tensor(to[:, :, 2 * C:3 * C], tiles(res), to[:, :, C:2 * C], ALU.subtract))

                h_in = h2[1 - par][:, :]
                xb = xz = x[par]

                def hot(g, k):
                    if k > 1:
                        dve.wait_ge(gat_full, g * GAT + max(k - 1, 1))
                    step(v.tensor_scalar(one_hot[k % 2][:, :], pos_t[:, :], float(k), None, ALU.is_equal))
                    (x_at if k <= EARLY else y_at)(f"hot{k}")

                def layer0():
                    dve.wait_ge(root_ready, b + 1)
                    step(v.reciprocal(d0, root))
                    step(v.tensor_scalar(root, root, 1e-7, None, ALU.add))
                    step(v.reciprocal(d1, root))
                    if a is not None:
                        narrow_sort.sort(1)
                    dve.wait_ge(misc_x, b * MISC_X + 1)
                    step(v.tensor_tensor(tiles(y), ps_misc[:, :].rearrange("p (t c) -> p t c", t=T), over_c(d0),
                                         ALU.mult))
                    split(0, b * 5 + 1, y, parts)
                    x_at("parts0")

                def layer0_end():
                    dve.wait_ge(prod_x, b * 4 + 1)
                    step(v.tensor_tensor(y[:, :], y[:, :], ps_prod[:, :], ALU.add))
                    step(v.scalar_tensor_tensor(tiles(y), tiles(y), 0.0, over_c(d0), ALU.max, ALU.mult))
                    step(v.tensor_tensor(xb[:, :], xb[:, :], y[:, :], ALU.add))
                    layer_norm(0, b * 3 + 2, xb, h, y)
                    x_at("h1")

                def propagate(i):
                    src = g_l1[:, :, DEPTH * C:(DEPTH + 1) * C] if i == 1 else tiles(y)
                    step(v.tensor_tensor(tiles(y), src, over_c(d1), ALU.mult))
                    split(0, b * 5 + 1 + i, y, parts)
                    x_at(f"parts{i}")

                def propagated(i):
                    dve.wait_ge(prod_x, b * 4 + 1 + i)
                    step(v.tensor_tensor(y[:, :], y[:, :], ps_prod[:, :], ALU.add))
                    step(v.tensor_tensor(tiles(y), tiles(y), over_c(d1), ALU.mult))
                    step(v.tensor_tensor(tiles(y), tiles(y), g_l1[:, :, (DEPTH - i) * C:(DEPTH - i + 1) * C],
                                         ALU.add))

                def rank(t):
                    dve.wait_ge(cum_full, b * CUM + t + 1)
                    v.tensor_tensor(rows(cum, t)[:, 0:HALF], ps_cum[:, 0:HALF], rows(adj_n, t)[:, 0:HALF],
                                    ALU.mult).then_inc(cum_read_v, 1)
                    v.tensor_copy(m_all[:, t:t + 1], ps_cum[:, N - 1:N])
                    v.tensor_tensor(rows(cum, t)[:, HALF:N], ps_cum[:, HALF:N], rows(adj_n, t)[:, HALF:N],
                                    ALU.mult).then_inc(cum_read_v, 1)

                slots_w_halves = [slots_w[:, i * WIDE * C:(i + 1) * WIDE * C] for i in range(2)]

                def wide_layer(layer, here, there):
                    d = 1 << layer
                    lower, upper, lo, hi = [half.rearrange("p (g x y) -> p g x y", x=2, y=d * C)[:, :, i]
                                            for half in (here, there) for i in range(2)]
                    st.done(v.tensor_tensor(lo, lower, upper, ALU.min))
                    step(v.tensor_tensor(hi, lower, upper, ALU.max))

                def narrow_sum(ranked):
                    for r, s in ranked:
                        w = over_c(w_rank[:, :, r])
                        if r == 0:
                            step(v.tensor_tensor(tiles(agg), tiles(s), w, ALU.mult))
                        else:
                            step(v.tensor_tensor(tiles(s), tiles(s), w, ALU.mult))
                            step(v.tensor_tensor(agg[:, :], agg[:, :], s, ALU.add))

                def keeps(tile_range):
                    for t in tile_range:
                        step(v.tensor_scalar(rows(keep, t), rows(cum, t), m_drop1[:, t:t + 1], None,
                                             ALU.not_equal))
                        step(v.scalar_tensor_tensor(rows(keep, t), rows(cum, t), m_drop2[:, t:t + 1],
                                                    rows(keep, t), ALU.not_equal, ALU.mult))
                        x_at(f"keep{t}")

                if a is not None:
                    hot(a, 4)
                    hot(a, 5)
                if c is not None:
                    dve.wait_ge(misc_z, c * MISC_Z + 3)
                    step(v.tensor_tensor(tiles(z), ps_misc[:, :].rearrange("p (t c) -> p t c", t=T),
                                         over_t(bias_l2[:, :]), ALU.add))
                    z_at("y_read")
                    step(v.tensor_tensor(tiles(z), tiles(z), over_c(mask[:, c, :]), ALU.mult))
                    step(v.tensor_tensor(xz[:, :], xz[:, :], z[:, :], ALU.add))
                    layer_norm(1, c + 1, xz, h, z)
                    z_at("h3")
                if a is not None:
                    hot(a, 6)
                if c is not None:
                    dve.wait_ge(misc_z, (c + 1) * MISC_Z)
                    step(v.tensor_copy(z[:, :], ps_misc[:, :]))
                    split(1, c + 1, z, parts)
                    z_at("parts_l3")
                    step(v.tensor_tensor(tiles(xz), tiles(xz), over_t(bias_l3[:, :]), ALU.add))
                if a is not None:
                    hot(a, 7)
                    dve.wait_ge(gat_full, a * GAT + SLOTS - 1)
                    for k in range(1, SLOTS):
                        step(v.tensor_scalar(hot_w(k), pos_w[:, :], float(k), None, ALU.is_equal))
                    y_at("hot_w_low")
                    dve.wait_ge(gat_full, a * GAT + SLOTS)
                    for k in range(SLOTS, WIDE):
                        step(v.tensor_scalar(hot_w(k), pos_w[:, :], float(k), None, ALU.is_equal))
                    y_at("hot_w_high")
                if c is not None:
                    dve.wait_ge(prod_z, c + 1)
                    step(v.tensor_tensor(xz[:, :], xz[:, :], ps_prod[:, :], ALU.add))
                    z_at("result")
                if b is not None:
                    dve.wait_ge(x_loaded, (b + 1) * 16)
                    layer_norm(0, b * 3 + 1, xb, h, y)
                    x_at("h0")
                if a is not None:
                    dve.wait_ge(gat_free, (a + 1) * GAT)
                    dve.wait_ge(weights_ready, a + 1)
                    slow_v(a, h_in)
                    y_at("slow_done")
                    narrow_sort = Sorter(NETWORK_8, [h_in] + slot[0:SLOTS - 1], slot[SLOTS - 1:], kept=h_in)
                    narrow_sort.sort(1)
                if b is not None:
                    layer0()
                    if a is not None:
                        dve.wait_ge(tables_ready, a + 1)
                for t in range(T):
                    if b is not None:
                        rank(t)
                    if a is not None:
                        if t % 2:
                            narrow_sort.sort(1)
                        else:
                            here, there = slots_w_halves[::-1 if t // 2 % 2 else 1]
                            wide_layer(t // 2, here, there)
                if a is not None:
                    narrow_sort.sort(len(narrow_sort.layers))
                    top = list(enumerate(narrow_sort.top()))
                    wide_sort = Sorter(NETWORK_16[4:], *[[half[:, i * C:(i + 1) * C] for i in range(WIDE)]
                                                         for half in slots_w_halves])
                if b is not None:
                    dve.wait_ge(misc_x, b * MISC_X + 2)
                    step(v.tensor_tensor(place[:, :], ps_misc[:, 0:T], wide[:, :], ALU.mult))
                    for t in range(T):
                        step(v.tensor_scalar(select[par][:, t, :], places[:, :], place[:, t:t + 1], None,
                                             ALU.is_equal))
                    x_at("select")
                    layer0_end()
                if a is not None:
                    narrow_sum(top[:4])
                if b is not None:
                    dve.wait_ge(thresholds_ready, b + 1)
                    dve.wait_ge(cum_read_v, 2 * (b + 1) * T)
                    keeps(range(T // 2))
                    dve.wait_ge(misc_x_act, (b + 1) * (T // 2))
                    propagate(1)
                    keeps(range(T // 2, T))
                if a is not None:
                    narrow_sum(top[4:])
                    y_at("narrow_done")
                if b is not None:
                    propagated(1)
                    propagate(2)
                    dve.wait_ge(tr_free, tr_x + 2 * T + 4)
                    for t in range(T):
                        step(v.tensor_tensor(rows(cum, t), rows(cum, t), rows(keep, t), ALU.mult))
                        step(v.tensor_tensor(rows(cum, t), rows(cum, t), rows(keep_t, t), ALU.mult))
                        x_at(f"pos{t}")
                    propagated(2)
                    propagate(3)
                if b is not None:
                    dve.wait_ge(tr_free, tr_x + 3 * T + 4)
                    step(v.tensor_scalar(valid_t[:, :], pos_t[:, :], 1.0, None, ALU.is_ge))
                    x_at("valid")
                    hot(b, 1)
                    propagated(3)
                    step(v.tensor_tensor(xb[:, :], xb[:, :], y[:, :], ALU.add))
                    step(v.tensor_tensor(tiles(xb), tiles(xb), over_t(bias_l1[:, :]), ALU.add))
                    layer_norm(0, b * 3 + 3, xb, h2[par], y)
                    split(0, b * 5 + 5, h2[par], parts_h2)
                    dve.wait_ge(cum_read_act, (b + 1) * 2)
                    x_at("parts_h2")
                if a is not None:
                    wide_sort.sort(2)
                if b is not None:
                    hot(b, 2)
                if a is not None:
                    wide_sort.sort(2)
                if b is not None:
                    hot(b, 3)
                if a is not None:
                    wide_sort.sort(2)
                    dve.wait_ge(weights_w_ready, a + 1)
                    for r, s in enumerate(wide_sort.top()):
                        if r == 0:
                            step(v.tensor_scalar(agg_w[:, :], s, w_rank_w[:, 0:1], None, ALU.mult))
                        else:
                            step(v.scalar_tensor_tensor(agg_w[:, :], s, w_rank_w[:, r:r + 1], agg_w[:, :],
                                                        ALU.mult, ALU.add))
                    step(v.tensor_copy(parts_w[:, 0:C], agg_w[:, :]))
                    step(v.tensor_tensor(rest_w[:, :], agg_w[:, :], parts_w[:, 0:C], ALU.subtract))
                    step(v.tensor_copy(parts_w[:, C:2 * C], rest_w[:, :]))
                    step(v.tensor_tensor(parts_w[:, 2 * C:3 * C], rest_w[:, :], parts_w[:, C:2 * C],
                                         ALU.subtract))
                    y_at("sorted_w")
                    dve.wait_ge(misc_y, a * MISC_Y + 2)
                    step(v.tensor_tensor(agg[:, :], agg[:, :], ps_misc[:, :], ALU.add))
                    step(v.tensor_tensor(agg[:, :], agg[:, :], h2[1 - par][:, :], ALU.add))
                    y_at("mlp_in")
                st.restart()

            run(dve, stretch)


_INS = ["x", "adj", "nodemask", "L0_gnn_kernel", "L1_gnn_W", "L1_gnn_b", "L2_gnn_W1", "L2_gnn_b1", "L2_gnn_W2",
        "L2_gnn_b2", "L3_gnn_weight", "L3_gnn_bias"]


def kernel(**inputs):
    import numpy as _np
    import concourse.bacc as _bacc
    from concourse import mybir as _mybir
    from concourse.bass_utils import run_bass_kernel_spmd as _run

    nc = _bacc.Bacc("TRN2", target_bir_lowering=False, num_devices=1)
    arrays, args = {}, []
    for name in _INS:
        a = _np.ascontiguousarray(inputs[name])
        if a.dtype == _np.bool_:
            a = a.view(_np.uint8)
        arrays[f"in_{name}"] = a
        args.append(nc.dram_tensor(f"in_{name}", a.shape, _mybir.dt.from_np(a.dtype), kind="ExternalInput").ap())
    shape = inputs["x"].shape
    out = nc.dram_tensor("out", shape, _mybir.dt.float32, kind="ExternalOutput").ap()
    gnn_stack(nc, *args, out)
    r = _run(nc, [arrays], core_ids=[0])
    return r.results[0]["out"]
```
